# Optimizing a Trainium2 kernel written in Bass

```python
import numpy as np
import jax
import jax.numpy as jnp

def _softmax(x, axis=-1):
    return jax.nn.softmax(x, axis=axis)

def _gelu(x):
    return jax.nn.gelu(x, approximate=True)

def _silu(x):
    return jax.nn.silu(x)

def _sigmoid(x):
    return jax.nn.sigmoid(x)

def _layernorm(x, axis=-1, eps=1e-05):
    m = jnp.mean(x, axis=axis, keepdims=True)
    v = jnp.var(x, axis=axis, keepdims=True)
    return (x - m) / jnp.sqrt(v + eps)

def _scatter_add(tgt, idx, src, axis=0):
    return tgt.at[idx].add(src)

def _segment_sum(src, seg, n):
    return jax.ops.segment_sum(src, seg, n)
kernel_name = 'mk_xattn_ffn_d1_seqx_r8_2c93f0'

def setup_inputs(seed: int=0):
    np.random.seed(seed)
    _w = jnp.asarray

    def _rec_inputs():
        import jax
        import jax.numpy as jnp
        _rk = jax.random.key(seed)
        x = 7.22e-05 + 1 * jax.random.normal(jax.random.fold_in(_rk, 1), (16, 128, 256), jnp.float32)
        _lenS = 128 - jax.random.randint(jax.random.fold_in(_rk, 7), (16,), 0, max(1, 128 // 4) + 1, jnp.int32)
        _lenS2 = 128 - jax.random.randint(jax.random.fold_in(_rk, 8), (16,), 0, max(1, 128 // 4) + 1, jnp.int32)
        _ctx_512P = jax.random.normal(jax.random.fold_in(_rk, 11), (16, 16, 64), jnp.float32)
        _ctx_512c = jax.random.dirichlet(jax.random.fold_in(_rk, 511), 0.3 * jnp.ones((16,), jnp.float32), (16, 128))
        _ctx_512t = jnp.einsum('bsk,bkd->bsd', _ctx_512c, _ctx_512P)
        _ctx_512t = _ctx_512t * jax.lax.rsqrt(jnp.mean(jnp.square(_ctx_512t)) + 1e-12) * 0.953939
        ctx_512 = -0.000514642 + 1.00011 * (_ctx_512t + 0.3 * jax.random.normal(jax.random.fold_in(_rk, 611), (16, 128, 64), jnp.float32))
        return (x, ctx_512)
    x, ctx_512 = _rec_inputs()

    def _L0_xattn_setup():
        import jax, jax.numpy as jnp
        import numpy as np
        import math
        D_MODEL = 256
        N_HEADS = 16
        N_GROUPS = 4
        HEADS_PER_GROUP = N_HEADS // N_GROUPS
        HEAD_DIM = D_MODEL // N_HEADS
        B, S = (2, 256)
        key = jax.random.key(seed)
        k1, k2, k3, k4, k5 = jax.random.split(key, 5)
        q = jax.random.normal(k1, (B, S, D_MODEL), dtype=jnp.float32)
        k = jax.random.normal(k2, (B, S, N_GROUPS * HEAD_DIM), dtype=jnp.float32)
        v = jax.random.normal(k3, (B, S, N_GROUPS * HEAD_DIM), dtype=jnp.float32)
        lim = 1.0 / math.sqrt(D_MODEL)
        Wc = jax.random.uniform(k4, (D_MODEL, D_MODEL), minval=-lim, maxval=lim, dtype=jnp.float32)
        bc = jax.random.uniform(k5, (D_MODEL,), minval=-lim, maxval=lim, dtype=jnp.float32)
        return {'q': q, 'k': k, 'v': v, 'Wc': Wc, 'bc': bc}
    _L0_xattn_all = _L0_xattn_setup()
    _L0_xattn_in = {k: v for k, v in _L0_xattn_all.items() if k in ('Wc', 'bc')}
    del _L0_xattn_all

    def _L0_ffn_setup():
        import jax, jax.numpy as jnp
        import numpy as np
        BITS = 4
        SIGNED_MIN, SIGNED_MAX = (-2 ** (BITS - 1), 2 ** (BITS - 1) - 1)
        UNSIGNED_MIN, UNSIGNED_MAX = (0, 2 ** BITS - 1)
        INT32_MIN, INT32_MAX = (-2.0 ** 31, 2.0 ** 31 - 1)

        def fake_quant(x, scale, qmin, qmax):
            q = jnp.clip(jnp.round(x / scale), qmin, qmax) * scale
            return x + jax.lax.stop_gradient(q - x)

        def weight_scale(W):
            return jax.lax.stop_gradient(jnp.max(jnp.abs(W))) / SIGNED_MAX
        key = jax.random.key(seed)
        ks = jax.random.split(key, 5)
        B, S, D, F = (4, 256, 256, 1024)
        return {'x': jax.random.normal(ks[0], (B, S, D), dtype=jnp.float32), 'W1': jax.random.normal(ks[1], (F, D), dtype=jnp.float32) * 0.02, 'b1': jax.random.normal(ks[2], (F,), dtype=jnp.float32) * 0.02, 'W2': jax.random.normal(ks[3], (D, F), dtype=jnp.float32) * 0.02, 'b2': jax.random.normal(ks[4], (D,), dtype=jnp.float32) * 0.02, 's_act1': jnp.full((1,), 0.1, dtype=jnp.float32), 's_act2': jnp.full((1,), 0.1, dtype=jnp.float32)}
    _L0_ffn_all = _L0_ffn_setup()
    _L0_ffn_in = {k: v for k, v in _L0_ffn_all.items() if k in ('W1', 'b1', 'W2', 'b2', 's_act1', 's_act2')}
    del _L0_ffn_all
    return {'x': x, 'ctx_512': ctx_512, 'L0_xattn_Wc': _L0_xattn_in['Wc'], 'L0_xattn_bc': _L0_xattn_in['bc'], 'L0_ffn_W1': _L0_ffn_in['W1'], 'L0_ffn_b1': _L0_ffn_in['b1'], 'L0_ffn_W2': _L0_ffn_in['W2'], 'L0_ffn_b2': _L0_ffn_in['b2'], 'L0_ffn_s_act1': _L0_ffn_in['s_act1'], 'L0_ffn_s_act2': _L0_ffn_in['s_act2']}

def reference(x, ctx_512, L0_xattn_Wc, L0_xattn_bc, L0_ffn_W1, L0_ffn_b1, L0_ffn_W2, L0_ffn_b2, L0_ffn_s_act1, L0_ffn_s_act2):
    import jax
    import jax.numpy as jnp

    def _L0_xattn_ref(q, k, v, Wc, bc):
        import jax, jax.numpy as jnp
        import numpy as np
        import math
        D_MODEL = 256
        N_HEADS = 16
        N_GROUPS = 4
        HEADS_PER_GROUP = N_HEADS // N_GROUPS
        HEAD_DIM = D_MODEL // N_HEADS
        B, S = (2, 256)
        b, s, _ = q.shape
        qh = q.reshape(b, s, N_GROUPS, HEADS_PER_GROUP, HEAD_DIM).transpose(0, 2, 3, 1, 4)
        kh = k.reshape(b, s, N_GROUPS, HEAD_DIM).transpose(0, 2, 1, 3)
        vh = v.reshape(b, s, N_GROUPS, HEAD_DIM).transpose(0, 2, 1, 3)
        scale = 1.0 / math.sqrt(HEAD_DIM)
        scores = jnp.einsum('bghsd,bgtd->bghst', qh, kh) * scale
        probs = jax.nn.softmax(scores, axis=-1)
        out = jnp.einsum('bghst,bgtd->bghsd', probs, vh)
        out = out.transpose(0, 3, 1, 2, 4).reshape(b, s, D_MODEL)
        return out @ Wc.T + bc

    def _L0_ffn_ref(x, W1, b1, W2, b2, s_act1, s_act2):
        import jax, jax.numpy as jnp
        import numpy as np
        BITS = 4
        SIGNED_MIN, SIGNED_MAX = (-2 ** (BITS - 1), 2 ** (BITS - 1) - 1)
        UNSIGNED_MIN, UNSIGNED_MAX = (0, 2 ** BITS - 1)
        INT32_MIN, INT32_MAX = (-2.0 ** 31, 2.0 ** 31 - 1)

        def fake_quant(x, scale, qmin, qmax):
            q = jnp.clip(jnp.round(x / scale), qmin, qmax) * scale
            return x + jax.lax.stop_gradient(q - x)

        def weight_scale(W):
            return jax.lax.stop_gradient(jnp.max(jnp.abs(W))) / SIGNED_MAX
        s1 = s_act1[0]
        s2 = s_act2[0]
        x_q = fake_quant(x, s1, SIGNED_MIN, SIGNED_MAX)
        sw1 = weight_scale(W1)
        W1_q = fake_quant(W1, sw1, SIGNED_MIN, SIGNED_MAX)
        b1_q = fake_quant(b1, s1 * sw1, INT32_MIN, INT32_MAX)
        h = jnp.einsum('bsd,fd->bsf', x_q, W1_q) + b1_q
        h_q = fake_quant(jax.nn.relu(h), s2, UNSIGNED_MIN, UNSIGNED_MAX)
        sw2 = weight_scale(W2)
        W2_q = fake_quant(W2, sw2, SIGNED_MIN, SIGNED_MAX)
        b2_q = fake_quant(b2, s2 * sw2, INT32_MIN, INT32_MAX)
        out = jnp.einsum('bsf,df->bsd', h_q, W2_q) + b2_q
        return out
    x = x + _L0_xattn_ref(_layernorm(x, axis=-1), ctx_512, ctx_512, L0_xattn_Wc, L0_xattn_bc)
    x = x + _L0_ffn_ref(_layernorm(x, axis=-1), L0_ffn_W1, L0_ffn_b1, L0_ffn_W2, L0_ffn_b2, L0_ffn_s_act1, L0_ffn_s_act2)
    return x

_drawn_inputs = setup_inputs


def setup_inputs(seed=0):
    import zlib

    import numpy as np

    out = dict(_drawn_inputs(seed))
    spreads = {}
    factors = {'L0_ffn_b1': 3.858, 'L0_ffn_b2': 3.077}
    for name, (base, spread) in spreads.items():
        noise = np.random.default_rng([zlib.crc32(name.encode()), seed]).standard_normal(out[name].shape)
        drawn = base * np.exp(spread * noise) if base else spread * noise
        out[name] = jnp.asarray(drawn.astype(out[name].dtype))
    for name, factor in factors.items():
        out[name] = (out[name] * factor).astype(out[name].dtype)
    return out
```

```python
import concourse.bass as bass
from concourse import mybir
from contextlib import ExitStack


def xattn_ffn(nc, x, ctx_512, Wc, bc, W1, b1, W2, b2, s_act1, s_act2, out):
    f32, bf16 = mybir.dt.float32, mybir.dt.bfloat16
    RMAX = bass.bass_isa.ReduceOp.max
    ALU, ACT, AX = mybir.AluOpType, mybir.ActivationFunctionType, mybir.AxisListType

    NB, S, D = x.shape
    DK = ctx_512.shape[2]
    F = W1.shape[0]
    H, G = 16, 4
    HD = D // H
    HG = H // G
    NH = H + G
    W = D + DK
    COMBO = 6
    KR = COMBO * HD
    KM = KR + 2
    DH = D // 128
    NF = F // 128
    RING = 4
    LAST = 4
    NG = 4
    BG = NB // NG
    TG = BG * S
    EPS = 1e-5
    MAGIC = 1.5 * 2.0 ** 23
    QMAX, QMIN, UMAX = 7.0, -8.0, 15.0
    IMAX = 2.0 ** 22

    es = ExitStack()
    with es:
        def sb(name, shape, dt):
            return es.enter_context(nc.sbuf_tensor(name, shape, dt))

        def sem(name):
            return es.enter_context(nc.semaphore(name))

        X = sb("X", [S, NB, D], f32)
        QK = sb("QK", [S, NB + 1, W], f32)
        X1 = sb("X1", [S, NB, D], f32)
        Y = sb("Y", [S, NB, D], bf16)
        PARTS = sb("PARTS", [S, 2, NH, COMBO, HD], bf16)
        REST = sb("REST", [S, 2, W], f32)
        QS = sb("QS", [KM, RING, H, S], bf16)
        KS = sb("KS", [KM, RING, G, S], bf16)
        NMAX = sb("NMAX", [S, 2, H], f32)
        NMP = sb("NMP", [S, 2, 2 * H], bf16)
        NMT = sb("NMT", [2 * H, 2, S], bf16)
        V1 = sb("V1", [S, 2, G, 32], f32)
        PR = sb("PR", [S, 2, G, HG * S], f32)
        OT = sb("OT", [128, HG * S], f32)
        RSUM = sb("RSUM", [S, H], f32)
        ON = sb("ON", [S, G, HG, HD], f32)
        ONT = sb("ONT", [128, DH, S], f32)
        ST1 = sb("ST1", [S, NB, 6], f32)
        MV1 = sb("MV1", [S, NB, 2], f32)
        RS1 = sb("RS1", [S, NB], f32)
        VE1 = sb("VE1", [S, NB], f32)
        ST2 = sb("ST2", [S, RING, 6], f32)
        MV2 = sb("MV2", [S, RING, 2], f32)
        VE2 = sb("VE2", [S, RING], f32)
        RS2 = sb("RS2", [S, RING], f32)
        RQ2 = sb("RQ2", [S, RING], f32)
        YA = sb("YA", [S, 2, D], f32)
        YB = sb("YB", [S, 2, D], f32)
        HALF = sb("HALF", [S, NB], f32)
        IDF = sb("IDF", [128, 128], f32)
        IDB = sb("IDB", [128, 128], bf16)
        MAG = sb("MAG", [128, 1], f32)
        BC = sb("BC", [S, D], f32)
        B2 = sb("B2", [S, D], f32)
        B2Q = sb("B2Q", [S, D], f32)
        B1 = sb("B1", [128, NF], f32)
        B1Q = sb("B1Q", [128, NF], f32)
        SA = sb("SA", [128, 2], f32)
        SC = sb("SC", [128, 16], f32)
        WCR = sb("WCR", [128, DH, D], f32)
        WCT = sb("WCT", [128, DH, D], f32)
        W1R = sb("W1R", [128, NF, D], f32)
        W2R = sb("W2R", [128, DH, F], f32)
        W1Q = sb("W1Q", [128, NF, D], bf16)
        W2Q = sb("W2Q", [128, DH, F], bf16)
        W1T = sb("W1T", [128, DH, F], bf16)
        W2T = sb("W2T", [128, NF, D], bf16)
        YT = sb("YT", [128, 2, DH, TG], bf16)
        HF = sb("HF", [128, 2, TG], f32)
        HM = sb("HM", [128, 2, TG], f32)
        HQ = sb("HQ", [128, 2, NF, TG], bf16)
        OUT = sb("OUT", [S, 2, BG, D], f32)
        TB1 = sb("TB1", [128, NF], f32)
        TB2 = sb("TB2", [S, D], f32)
        AMAX = sb("AMAX", [128, 2], f32)
        EPST = sb("EPST", [128, 1], f32)
        WARM = sb("WARM", [128, 1], f32)

        def bank(name):
            return es.enter_context(nc.psum_tensor(name, [128, 512], f32))
        P_MAX = [bank("P_MAX0"), bank("P_MAX1")]
        P_EXP = [bank("P_EXP0"), bank("P_EXP1")]
        P_QT = bank("P_QT")
        P_KT = bank("P_KT")
        P_AT = bank("P_AT")
        P_PJ = bank("P_PJ")

        P_H = [P_MAX[0], P_MAX[1], P_EXP[0]]
        P_O = [P_AT, P_PJ]
        P_YT = P_QT

        def as_bf16(t):
            return t[:, :].bitcast(bf16)

        x_in = [sem(f"x_in{c}") for c in range(5)]
        ctx_in = [sem(f"ctx_in{c}") for c in range(2)]
        bc_in, wc_in, w1_in, w2_in, small_in = sem("bc_in"), sem("wc_in"), sem("w1_in"), sem("w2_in"), sem("small_in")
        zeroed, consts_ready = sem("zeroed"), sem("consts_ready")
        ones_done = sem("ones_done")
        st1_done, mv1_done, ve1_done, rs1_done, q_done = (sem(n) for n in ("st1_done", "mv1_done", "ve1_done", "rs1_done", "q_done"))
        part1_done, rest_done, part2_done, part3_done = (sem(n) for n in ("part1_done", "rest_done", "part2_done", "part3_done"))
        xb_done, v1_done = sem("xb_done"), sem("v1_done")
        qt_done, qs0_done, qs1_done = sem("qt_done"), sem("qs0_done"), sem("qs1_done")
        kt_done, ks_done = sem("kt_done"), sem("ks_done")
        smax_done, max_done, nmp1_done, nmp2_done = sem("smax_done"), sem("max_done"), sem("nmp1_done"), sem("nmp2_done")
        nmt_done, nmts_done = sem("nmt_done"), sem("nmts_done")
        nm_row = [sem("nm_row0"), sem("nm_row1")]
        sexp_done, exp_done, at_done, ats_done = sem("sexp_done"), sem("exp_done"), sem("at_done"), sem("ats_done")
        back_done, rsum_done, on_done, ont_done, onts_done = (sem(n) for n in ("back_done", "rsum_done", "on_done", "ont_done", "onts_done"))
        proj_done, x1_done, st2_done, mv2_done = sem("proj_done"), sem("x1_done"), sem("st2_done"), sem("mv2_done")
        ve2_done, rs2_done, rq2_done = sem("ve2_done"), sem("rs2_done"), sem("rq2_done")
        ya_done, yb_done, y_done = sem("ya_done"), sem("yb_done"), sem("y_done")
        wct_done, wcts_done = sem("wct_done"), sem("wcts_done")
        amax_done, amaxall_done, scales = sem("amax_done"), sem("amaxall_done"), sem("scales")
        wm_done, wq_done, wt_done, wts_done = sem("wm_done"), sem("wq_done"), sem("wt_done"), sem("wts_done")
        x1b_done, warm_done = sem("x1b_done"), sem("warm_done")
        yt_done, yts_done, h_done, relu_done, hm_done, hq_done = (sem(n) for n in ("yt_done", "yts_done", "h_done", "relu_done", "hm_done", "hq_done"))
        o_done, res_done = sem("o_done"), sem("res_done")
        out_sent = [sem("out_sent0"), sem("out_sent1")]

        CH = [(0, 1), (1, 4), (4, 8), (8, 12), (12, 16)]
        CC = [(0, 4), (4, 16)]
        AMX, AMA, RMX, SW, S1SW, RS1SW, CH_, S2SW, RS2SW, RSA1, RSA2 = 0, 1, 2, 4, 6, 7, 8, 9, 10, 11, 12

        QH, KH = slice(0, H), slice(H, NH)
        QSLOTS = {1: (QH, slice(0, 3)), 2: (QH, slice(3, 5)), 3: (QH, slice(5, 6))}
        KSLOTS = {1: (KH, slice(1, 6, 2)), 2: (KH, slice(0, 5, 4)), 3: (KH, slice(2, 3))}

        def static(b):
            return isinstance(b, int)

        def there(b, first=0, last=NB - 1):
            return not static(b) or first <= b <= last

        def wait(eng, s, value):
            if not static(value) or value > 0:
                eng.wait_ge(s, value)

        def pipeline(eng, step, head=None):
            head = head or (lambda it, u: None)
            for it in range(LAST):
                head(it, it)
                step(it, it)
            head(LAST, 0)
            with eng.Fori(LAST // RING, NB // RING) as k:
                for u in range(RING):
                    step(k * RING + u, u)
                    head(k * RING + u + 1, (u + 1) % RING)
            for it in range(NB, NB + LAST):
                step(it, it % RING)
                head(it + 1, (it + 1) % RING)

        def nm_rows(it, u, lag):
            return (it - u) * 16 + 32 * ((u - lag) // 2 + 1)

        block = es.enter_context(nc.Block())

        @block.sync
        def _(sp):
            def load_x(c):
                a, b = CH[c]
                sp.dma_start(X[:, a:b, :], x[a:b].rearrange("b s d -> s b d")).then_inc(x_in[c], 16)

            def load_ctx(c):
                a, b = CC[c]
                sp.dma_start(QK[:, a:b, D:W], ctx_512[a:b].rearrange("b s d -> s b d")).then_inc(ctx_in[c], 16)
            load_x(0)
            load_ctx(0)
            load_x(1)
            sp.dma_start(BC[:, :], bc.rearrange("(a n) -> a n", a=1).to_broadcast([S, D])).then_inc(bc_in, 16)
            load_x(2)
            sp.dma_start(WCR[:, :, :], Wc.rearrange("(j p) k -> p j k", p=128)).then_inc(wc_in, 16)
            load_ctx(1)
            load_x(3)
            sp.dma_start(W1R[:, :, :], W1.rearrange("(j p) k -> p j k", p=128)).then_inc(w1_in, 16)
            load_x(4)
            sp.dma_start(W2R[:, :, :], W2.rearrange("(j p) k -> p j k", p=128)).then_inc(w2_in, 16)
            with nc.allow_non_contiguous_dma(reason="1024 biases, one to a partition and tile"):
                sp.dma_start(B1[:, :], b1.rearrange("(j p) -> p j", p=128)).then_inc(small_in, 16)
            sp.dma_start(B2[:, :], b2.rearrange("(a n) -> a n", a=1).to_broadcast([S, D])).then_inc(small_in, 16)
            sp.dma_start(SA[:, 0:1], s_act1.rearrange("(a n) -> a n", a=1).to_broadcast([128, 1])).then_inc(small_in, 16)
            sp.dma_start(SA[:, 1:2], s_act2.rearrange("(a n) -> a n", a=1).to_broadcast([128, 1])).then_inc(small_in, 16)

            def step(it, u):
                b, r = it - 2, (u - 2) % RING
                if there(b):
                    sp.wait_ge(nmts_done, b + 1)
                    for part in range(2):
                        sp.dma_start(QS[KR + part:KR + part + 1, r, :, :],
                                     NMT[part * H:part * H + H, r % 2, :]).then_inc(nm_row[r % 2], 16)
            pipeline(sp, step)

            for n in range(NG):
                sp.wait_ge(res_done, BG * (n + 1))
                sp.dma_start(out[n * BG:(n + 1) * BG].rearrange("b s d -> s b d"),
                             OUT[:, n % 2, :, :]).then_inc(out_sent[n % 2], 16)
            sp.wait_ge(out_sent[0], 16 * (NG // 2))
            sp.wait_ge(out_sent[1], 16 * (NG // 2))

        @block.gpsimd
        def _(pool):
            pool.memset(HALF[:, :], -0.5).then_inc(zeroed, 1)
            pool.memset(EPST[:, :], EPS).then_inc(zeroed, 1)
            pool.memset(IDF[:, :], 0.0).then_inc(zeroed, 1)
            pool.memset(IDB[:, :], 0.0).then_inc(zeroed, 1)
            pool.memset(MAG[:, :], MAGIC).then_inc(consts_ready, 1)
            pool.wait_ge(zeroed, 4)
            for t in (IDF, IDB):
                pool.affine_select(out=t[:, :], in_=t[:, :], compare_op=ALU.not_equal, fill=1.0, base=0,
                                   pattern=[[-1, 128]], channel_multiplier=1).then_inc(consts_ready, 1)

            def rstd1(c):
                a, b = CH[c]
                pool.wait_ge(mv1_done, b)
                pool.tensor_scalar(VE1[:, a:b], MV1[:, a:b, 1], EPS, float(HD), ALU.add, ALU.mult).then_inc(ve1_done, 1)
                pool.wait_ge(ve1_done, c + 1)
                pool.tensor_tensor(RS1[:, a:b], VE1[:, a:b], HALF[:, a:b], ALU.pow).then_inc(rs1_done, 1)

            rstd1(0)
            pool.memset(V1[:, :, :, HD:32], 0.0).then_inc(zeroed, 1)
            pool.wait_ge(zeroed, 5)
            pool.memset(V1[:, :, :, HD:HD + 1], 1.0).then_inc(v1_done, 1)
            rstd1(1)

            def rest(b, r):
                pool.wait_ge(part1_done, 2 * (b + 1))
                wait(pool, part3_done, 2 * (b - 1))
                pool.tensor_tensor(REST[:, r % 2, :].rearrange("p (h d) -> p h d", d=HD),
                                   QK[:, b, :].rearrange("p (h d) -> p h d", d=HD),
                                   PARTS[:, r % 2, :, 1, :], ALU.subtract).then_inc(rest_done, 1)

            def part3(b, r):
                pool.wait_ge(part2_done, 2 * (b + 1))
                rest_ = REST[:, r % 2, :].rearrange("p (h d) -> p h d", d=HD)
                for hs, slot in QSLOTS[3], KSLOTS[3]:
                    pool.tensor_tensor(PARTS[:, r % 2, hs, slot, :], rest_[:, hs, :].unsqueeze(2), PARTS[:, r % 2, hs, 4:5, :],
                                       ALU.subtract).then_inc(part3_done, 1)

            rest(0, 0)
            part3(0, 0)
            pool.wait_ge(bc_in, 16)

            def step(it, u):
                if static(it) and it + 2 < len(CH):
                    rstd1(it + 2)
                if static(it) and it == NB:
                    pool.wait_ge(amax_done, 2)
                    pool.partition_all_reduce(AMAX[:, :], SC[:, AMX:AMX + 2], 128, RMAX).then_inc(amaxall_done, 2)
                if there(it + 1, 0, NB):
                    rest(it + 1, (u + 1) % RING)
                if there(it):
                    pool.wait_ge(q_done, it + 1)
                    pool.tensor_tensor(X[:, it, :], X[:, it, :], BC[:, :], ALU.add).then_inc(xb_done, 1)
                if there(it - 2):
                    b, r = it - 2, (u - 2) % RING
                    wait(pool, at_done, b - 1)
                    pool.wait_ge(ctx_in[0 if static(b) and b < CC[0][1] else 1], 16)
                    pool.tensor_copy(V1[:, r % 2, :, 0:HD],
                                     QK[:, b, D:W].rearrange("p (g d) -> p g d", g=G)).then_inc(v1_done, 1)
                if there(it + 1, 0, NB):
                    part3(it + 1, (u + 1) % RING)
                if there(it - 4):
                    b, r = it - 4, (u - 4) % RING
                    pool.wait_ge(mv2_done, b + 1)
                    pool.tensor_tensor(VE2[:, r:r + 1], MV2[:, r, 1:2], EPST[:, :], ALU.add).then_inc(ve2_done, 1)
                    pool.wait_ge(ve2_done, b + 1)
                    pool.tensor_tensor(RS2[:, r:r + 1], VE2[:, r:r + 1], HALF[:, 0:1], ALU.pow).then_inc(rs2_done, 1)
                    if static(b) and b == 0:
                        pool.wait_ge(scales, 1)
                    pool.wait_ge(rs2_done, b + 1)
                    pool.tensor_tensor(RQ2[:, r:r + 1], RS2[:, r:r + 1], SC[:, RSA1:RSA1 + 1], ALU.mult).then_inc(rq2_done, 1)
            pipeline(pool, step)
            pool.wait_ge(scales, 23)
            for b in range(NB):
                pool.wait_ge(y_done, b + 1)
                pool.tensor_tensor(X1[:, b, :], X1[:, b, :], B2Q[:, :], ALU.add).then_inc(x1b_done, 1)

        @block.vector
        def _(dve):
            vec = nc.vector
            vec.memset(KS[KR:KM, :, :, :], 1.0).then_inc(ones_done, 1)

            def stats1(c):
                a, b = CH[c]
                dve.wait_ge(x_in[c], 16)
                for i in range(a, b):
                    vec.bn_stats(ST1[:, i, :], X[:, i, :]).then_inc(st1_done, 1)
                for i in range(a, b):
                    dve.wait_ge(st1_done, i + 1)
                    vec.bn_aggr(MV1[:, i, :], ST1[:, i, :]).then_inc(mv1_done, 1)

            def norm1(c):
                a, b = CH[c]
                dve.wait_ge(rs1_done, c + 1)
                for i in range(a, b):
                    vec.tensor_scalar(QK[:, i, 0:D], X[:, i, :], MV1[:, i, 0:1], RS1[:, i:i + 1],
                                      ALU.subtract, ALU.mult).then_inc(q_done, 1)

            def small(ins, n):
                ins.then_inc(scales, 1)
                dve.wait_ge(scales, n)

            stats1(0)
            stats1(1)
            norm1(0)
            norm1(1)
            dve.wait_ge(small_in, 64)
            small(vec.reciprocal(SC[:, RSA1:RSA1 + 2], SA[:, 0:2]), 1)
            dve.wait_ge(wct_done, 1)
            vec.tensor_copy(WCT[:, :, :], P_PJ[:, :].rearrange("p (j n) -> p j n", j=DH)).then_inc(wcts_done, 1)

            def row_max(b, r, g):
                i = b * HG + g
                dve.wait_ge(smax_done, i + 1)
                if g == 0:
                    wait(dve, nmp2_done, b - 1)
                vec.tensor_reduce(NMAX[:, r % 2, g * HG:(g + 1) * HG],
                                  P_MAX[g % 2][:, :].rearrange("p (h t) -> p h t", t=S),
                                  AX.X, ALU.max, negate=True).then_inc(max_done, 1)

            def round_any(dst, src, n):
                small(vec.tensor_scalar(dst[0], src, IMAX, -IMAX, ALU.min, ALU.max), n)
                small(vec.tensor_tensor(dst[1], src, dst[0], ALU.subtract), n + 1)
                small(vec.tensor_scalar(dst[0], dst[0], MAGIC, MAGIC, ALU.add, ALU.subtract), n + 2)
                small(vec.tensor_tensor(dst[1], dst[1], dst[0], ALU.add), n + 3)

            def head(it, u):
                if there(it - 4):
                    b = it - 4
                    dve.wait_ge(back_done, b + 1)
                    back = P_AT[:, :].rearrange("p (h g e) -> p h g e", h=HG, g=G)
                    vec.reciprocal(RSUM[:, :].rearrange("p (h g) -> p h g", h=HG), back[:, :, :, HD]).then_inc(rsum_done, 1)
                    dve.wait_ge(rsum_done, b + 1)
                    wait(dve, ont_done, b)
                    vec.tensor_tensor(ON[:, :, :, :].rearrange("p g h d -> p h g d"), back[:, :, :, 0:HD],
                                      RSUM[:, :].rearrange("p (h g) -> p h g", h=HG).unsqueeze(3).to_broadcast([S, HG, G, HD]),
                                      ALU.mult).then_inc(on_done, 1)
                if there(it - 5) and not (static(it) and it == LAST):
                    b, r = it - 5, (u - 5) % RING
                    dve.wait_ge(rq2_done, b + 1)
                    wait(dve, yb_done, b)
                    vec.tensor_scalar(YA[:, r % 2, :], X1[:, b, :], MV2[:, r, 0:1], RQ2[:, r:r + 1],
                                      ALU.subtract, ALU.mult).then_inc(ya_done, 1)
                    dve.wait_ge(ya_done, b + 1)
                    wait(dve, y_done, b)
                    vec.tensor_scalar(YB[:, r % 2, :], YA[:, r % 2, :], QMAX, QMIN, ALU.min, ALU.max).then_inc(yb_done, 1)
                    dve.wait_ge(yb_done, b + 1)
                    vec.tensor_scalar(Y[:, b, :], YB[:, r % 2, :], MAGIC, MAGIC, ALU.add, ALU.subtract).then_inc(y_done, 1)

            def step(it, u):
                if there(it):
                    r = u % RING
                    dve.wait_ge(qt_done, 2 * it + 1)
                    wait(dve, sexp_done, G * (it - RING + 1))
                    vec.tensor_copy(QS[0:KR, r, 0:H // 2, :],
                                    as_bf16(P_QT)[0:KR, :].rearrange("p (h s) -> p h s", s=S)).then_inc(qs0_done, 1)
                if there(it - 1):
                    for g in (0, 1):
                        row_max(it - 1, (u - 1) % RING, g)
                if there(it):
                    dve.wait_ge(kt_done, it + 1)
                    wait(dve, sexp_done, G * (it - RING + 1))
                    vec.tensor_copy(KS[0:KR, r, :, :], as_bf16(P_KT)[0:KR, 0:G * S].rearrange("p (g t) -> p g t", t=S)).then_inc(ks_done, 1)
                if there(it - 4):
                    b, r = it - 4, (u - 4) % RING
                    dve.wait_ge(proj_done, b + 1)
                    dve.wait_ge(xb_done, b + 1)
                    vec.tensor_tensor(X1[:, b, :], P_PJ[:, D:2 * D], X[:, b, :], ALU.add).then_inc(x1_done, 1)
                    dve.wait_ge(x1_done, b + 1)
                if there(it - 1):
                    row_max(it - 1, (u - 1) % RING, 2)
                if there(it - 4):
                    b, r = it - 4, (u - 4) % RING
                    vec.bn_stats(ST2[:, r, :], X1[:, b, :]).then_inc(st2_done, 1)
                    if not (static(it) and it == LAST):
                        wait(dve, y_done, b - RING + 1) if static(b) else None
                    dve.wait_ge(st2_done, b + 1)
                if there(it - 1):
                    row_max(it - 1, (u - 1) % RING, 3)
                if there(it - 4):
                    vec.bn_aggr(MV2[:, r, :], ST2[:, r, :]).then_inc(mv2_done, 1)
                if there(it - 1):
                    b, r = it - 1, (u - 1) % RING
                    dve.wait_ge(max_done, HG * (b + 1))
                    wait(dve, nmt_done, b - 1)
                    vec.tensor_copy(NMP[:, r % 2, 0:H], NMAX[:, r % 2, :]).then_inc(nmp1_done, 1)
                    dve.wait_ge(nmp1_done, b + 1)
                    vec.tensor_tensor(NMP[:, r % 2, H:2 * H], NMAX[:, r % 2, :], NMP[:, r % 2, 0:H],
                                      ALU.subtract).then_inc(nmp2_done, 1)
                if static(it):
                    if it + 2 < len(CH):
                        stats1(it + 2)
                        norm1(it + 2)
                    if it == 3:
                        vec.memset(QK[:, NB, :], 0.0).then_inc(q_done, 1)
                    if it == 1:
                        dve.wait_ge(w1_in, 16)
                        vec.tensor_reduce(SC[:, AMX:AMX + 1], W1R[:, :, :], AX.XY, ALU.max,
                                          apply_absolute_value=True).then_inc(amax_done, 1)
                    if it == 3:
                        dve.wait_ge(w2_in, 16)
                        vec.tensor_reduce(SC[:, AMX + 1:AMX + 2], W2R[:, :, :], AX.XY, ALU.max,
                                          apply_absolute_value=True).then_inc(amax_done, 1)
                    if it == NB:
                        weight_scales()
                    if it == NB + 1:
                        biases()
                    if it in (NB + 1, NB + 2):
                        w = it - NB - 1
                        dve.wait_ge(wm_done, w + 1)
                        src, dst = ((W1R, W1Q), (W2R, W2Q))[w]
                        vec.tensor_scalar(dst[:, :, :], src[:, :, :], MAGIC, 1.0, ALU.subtract, ALU.mult).then_inc(wq_done, 1)

            def weight_scales():
                dve.wait_ge(amaxall_done, 2)
                small(vec.reciprocal(SC[:, RMX:RMX + 2], AMAX[:, :]), 2)
                small(vec.tensor_scalar(SC[:, RMX:RMX + 2], SC[:, RMX:RMX + 2], QMAX, 1.0, ALU.mult, ALU.mult), 3)
                small(vec.tensor_scalar(SC[:, SW:SW + 2], AMAX[:, :], 1.0 / QMAX, 1.0, ALU.mult, ALU.mult), 4)
                small(vec.tensor_tensor(SC[:, S1SW:S1SW + 1], SA[:, 0:1], SC[:, SW:SW + 1], ALU.mult), 5)
                small(vec.tensor_tensor(SC[:, S2SW:S2SW + 1], SA[:, 1:2], SC[:, SW + 1:SW + 2], ALU.mult), 6)
                small(vec.reciprocal(SC[:, RS1SW:RS1SW + 1], SC[:, S1SW:S1SW + 1]), 7)
                small(vec.reciprocal(SC[:, RS2SW:RS2SW + 1], SC[:, S2SW:S2SW + 1]), 8)
                small(vec.tensor_tensor(SC[:, CH_:CH_ + 1], SC[:, S1SW:S1SW + 1], SC[:, RSA2:RSA2 + 1], ALU.mult), 9)

            def biases():
                small(vec.tensor_scalar(B1[:, :], B1[:, :], SC[:, RS1SW:RS1SW + 1], 1.0, ALU.mult, ALU.mult), 10)
                round_any((TB1[:, :], B1Q[:, :]), B1[:, :], 11)
                small(vec.tensor_scalar(B1Q[:, :], B1Q[:, :], 2.0 ** 31, -2.0 ** 31, ALU.min, ALU.max), 15)
                small(vec.tensor_scalar(B1Q[:, :], B1Q[:, :], SC[:, CH_:CH_ + 1], 1.0, ALU.mult, ALU.mult), 16)
                small(vec.tensor_scalar(B2[:, :], B2[:, :], SC[:, RS2SW:RS2SW + 1], 1.0, ALU.mult, ALU.mult), 17)
                round_any((TB2[:, :], B2Q[:, :]), B2[:, :], 18)
                small(vec.tensor_scalar(B2Q[:, :], B2Q[:, :], 2.0 ** 31, -2.0 ** 31, ALU.min, ALU.max), 22)
                small(vec.tensor_scalar(B2Q[:, :], B2Q[:, :], SC[:, S2SW:S2SW + 1], 1.0, ALU.mult, ALU.mult), 23)
            pipeline(dve, step, head)

            def quantise(n, f):
                i = n * NF + f
                dve.wait_ge(relu_done, i + 1)
                wait(dve, hq_done, i - 1)
                vec.tensor_scalar(HM[:, i % 2, :], HF[:, i % 2, :], UMAX, MAGIC, ALU.min, ALU.add).then_inc(hm_done, 1)
                dve.wait_ge(hm_done, i + 1)
                if f == 0:
                    wait(dve, o_done, BG * (n - 1))
                vec.tensor_scalar(HQ[:, n % 2, f, :], HM[:, i % 2, :], MAGIC, 1.0, ALU.subtract, ALU.mult).then_inc(hq_done, 1)

            def result(n, s):
                b = n * BG + s
                dve.wait_ge(o_done, b + 1)
                dve.wait_ge(x1b_done, b + 1)
                if s == 0 and n >= 2:
                    dve.wait_ge(out_sent[n % 2], 16 * (n // 2))
                vec.scalar_tensor_tensor(out=OUT[:, n % 2, s, :], in0=P_O[s % 2][:, 0:D], scalar=SC[:, S2SW:S2SW + 1],
                                         in1=X1[:, b, :], op0=ALU.mult, op1=ALU.add).then_inc(res_done, 1)

            for n in range(NG + 1):
                for f in range(NF):
                    if n < NG:
                        quantise(n, f)
                    if n >= 1 and f % 2 == 1:
                        result(n - 1, f // 2)


        @block.scalar
        def _(act):
            sc = nc.scalar

            def part1(b, r):
                act.wait_ge(q_done, b + 1)
                act.wait_ge(ctx_in[0 if static(b) and b < CC[0][1] else 1], 16)
                wait(act, qt_done, 2 * (b - 1))
                wait(act, kt_done, b - 1)
                spread(QK[:, b, :], r, 1, part1_done)

            def spread(value, r, part, done):
                value = value.rearrange("p (h d) -> p h d", d=HD)
                for hs, slots in QSLOTS[part], KSLOTS[part]:
                    to = PARTS[:, r % 2, hs, slots, :]
                    sc.copy(to, value[:, hs, :].unsqueeze(2).to_broadcast(list(to.shape))).then_inc(done, 1)

            def part2(b, r):
                act.wait_ge(rest_done, b + 1)
                spread(REST[:, r % 2, :], r, 2, part2_done)

            def exps(b, r, gs):
                for g in gs:
                    act.wait_ge(sexp_done, G * b + g + 1)
                    if g == 0:
                        wait(act, at_done, b - 1)
                    sc.activation(PR[:, r % 2, g, :], P_EXP[g % 2][:, :], ACT.Exp).then_inc(exp_done, 1)

            act.wait_ge(consts_ready, 1)
            sc.activation(WARM[:, :], MAG[:, :], ACT.Exp, scale=0.0).then_inc(warm_done, 1)
            part1(0, 0)
            part2(0, 0)

            def step(it, u):
                if there(it - 4):
                    b = it - 4
                    act.wait_ge(at_done, b + 1)
                    wait(act, back_done, b)
                    sc.copy(OT[:, :], P_AT[:, :]).then_inc(ats_done, 1)
                if there(it - 3):
                    exps(it - 3, (u - 3) % RING, (0, 1))
                if there(it - 2):
                    b, r = it - 2, (u - 2) % RING
                    act.wait_ge(nmt_done, b + 1)
                    wait(act, nm_row[r % 2], nm_rows(it, u, 4))
                    sc.copy(NMT[:, r % 2, :], as_bf16(P_KT)[0:2 * H, 0:S]).then_inc(nmts_done, 1)
                if there(it + 1, 0, NB):
                    part1(it + 1, (u + 1) % RING)
                if there(it - 3):
                    exps(it - 3, (u - 3) % RING, (2, 3))
                if there(it - 4):
                    b = it - 4
                    act.wait_ge(ont_done, b + 1)
                    wait(act, proj_done, b)
                    sc.copy(ONT[:, :, :], P_PJ[:, 0:D].rearrange("p (j s) -> p j s", j=DH)).then_inc(onts_done, 1)
                if there(it + 1, 0, NB):
                    part2(it + 1, (u + 1) % RING)
                if there(it):
                    r = u % RING
                    act.wait_ge(qt_done, 2 * it + 2)
                    wait(act, sexp_done, G * (it - RING + 1))
                    sc.copy(QS[0:KR, r, H // 2:H, :],
                            as_bf16(P_QT)[0:KR, :].rearrange("p (h s) -> p h s", s=S)).then_inc(qs1_done, 1)
                if static(it) and it in (NB, NB + 1):
                    w = it - NB
                    act.wait_ge(scales, 9)
                    t = (W1R, W2R)[w]
                    sc.activation(t[:, :, :], t[:, :, :], ACT.Identity, bias=MAG[:, 0:1],
                                  scale=SC[:, RMX + w:RMX + w + 1]).then_inc(wm_done, 1)
            pipeline(act, step)
            for w in range(2):
                for j in range(2):
                    i = 2 * w + j
                    act.wait_ge(wt_done, i + 1)
                    src = as_bf16(P_MAX[j])[:, :]
                    if w == 0:
                        sc.copy(W1T[:, j, :], src).then_inc(wts_done, 1)
                    else:
                        sc.copy(W2T[:, j * NF // 2:(j + 1) * NF // 2, :],
                                src.rearrange("p (f k) -> p f k", k=D)).then_inc(wts_done, 1)

            def turned(n):
                act.wait_ge(yt_done, n + 1)
                wait(act, h_done, NF * (n - 1))
                sc.copy(YT[:, n % 2, :, :], as_bf16(P_YT)[:, :].rearrange("p (j s) -> p j s", j=DH)).then_inc(yts_done, 1)

            turned(0)
            act.wait_ge(scales, 23)
            for n in range(NG):
                for f in range(NF):
                    i = n * NF + f
                    act.wait_ge(h_done, i + 1)
                    wait(act, hm_done, i - 1)
                    sc.activation(HF[:, i % 2, :], P_H[i % 3][:, :], ACT.Relu, bias=B1Q[:, f:f + 1],
                                  scale=SC[:, CH_:CH_ + 1]).then_inc(relu_done, 1)
                    if f == 4 and n + 1 < NG:
                        turned(n + 1)

        @block.tensor
        def _(pe):
            mm, tr = nc.tensor.matmul, nc.tensor.transpose

            def q_turn(b, r, half):
                for j in range(H // 2):
                    last = tr(as_bf16(P_QT)[0:KR, j * S:(j + 1) * S],
                              PARTS[:, r % 2, half * (H // 2) + j, :, :].rearrange("p c d -> p (c d)"), IDB[:, :])
                last.then_inc(qt_done, 1)

            def k_turn(b, r):
                for g in range(G):
                    last = tr(as_bf16(P_KT)[0:KR, g * S:(g + 1) * S],
                              PARTS[:, r % 2, H + g, :, :].rearrange("p c d -> p (c d)"), IDB[:, :])
                last.then_inc(kt_done, 1)

            def scores_max(b, r, g):
                i = HG * b + g
                wait(pe, max_done, i - 1)
                for hh in range(HG):
                    last = mm(P_MAX[g % 2][:, hh * S:(hh + 1) * S], QS[0:KR, r, g * HG + hh, :], KS[0:KR, r, g, :],
                              start=True, stop=True)
                last.then_inc(smax_done, 1)

            def scores_exp(b, r, g):
                i = HG * b + g
                wait(pe, exp_done, i - 1)
                mm(P_EXP[g % 2][:, :], KS[:, r, g, :], QS[:, r, g * HG:(g + 1) * HG, :],
                   start=True, stop=True).then_inc(sexp_done, 1)

            pe.wait_ge(consts_ready, 3)
            pe.wait_ge(wc_in, 16)
            for j in range(DH):
                for m in range(DH):
                    last = tr(P_PJ[:, j * D + m * 128:j * D + (m + 1) * 128], WCR[:, m, j * 128:(j + 1) * 128], IDF[:, :])
            last.then_inc(wct_done, 1)

            def step(it, u):
                b1_, b2_, b3_, b4_ = (it - l for l in (1, 2, 3, 4))
                r1, r2, r3, r4 = ((u - l) % RING for l in (1, 2, 3, 4))
                if there(b3_):
                    if static(b3_) and b3_ == 0:
                        pe.wait_ge(ones_done, 1)
                    pe.wait_ge(nm_row[r3 % 2], nm_rows(it, u, 3))
                    for g in (0, 1):
                        scores_exp(b3_, r3, g)
                if there(b4_):
                    pe.wait_ge(ats_done, b4_ + 1)
                    for hh in range(HG):
                        last = tr(P_AT[:, hh * S:(hh + 1) * S], OT[:, hh * S:(hh + 1) * S], IDF[:, :])
                    last.then_inc(back_done, 1)
                if there(b1_):
                    pe.wait_ge(ks_done, b1_ + 1)
                    pe.wait_ge(qs0_done, b1_ + 1)
                    for g in (0, 1):
                        scores_max(b1_, r1, g)
                if there(b2_):
                    pe.wait_ge(nmp2_done, b2_ + 1)
                    wait(pe, nmts_done, b2_)
                    tr(as_bf16(P_KT)[0:2 * H, 0:S], NMP[:, r2 % 2, :], IDB[:, :]).then_inc(nmt_done, 1)
                if there(it):
                    pe.wait_ge(part3_done, 2 * (it + 1))
                    wait(pe, qs1_done, it)
                    q_turn(it, u, 0)
                if there(b3_):
                    for g in (2, 3):
                        scores_exp(b3_, r3, g)
                if there(b4_):
                    pe.wait_ge(on_done, b4_ + 1)
                    wait(pe, x1_done, b4_)
                    if static(b4_) and b4_ == 0:
                        pe.wait_ge(wcts_done, 1)
                    on = ON[:, :, :, :].rearrange("p g h d -> p (g h d)")
                    for j in range(DH):
                        last = tr(P_PJ[:, j * S:(j + 1) * S], on[:, j * 128:(j + 1) * 128], IDF[:, :])
                    last.then_inc(ont_done, 1)
                if there(it):
                    wait(pe, nmts_done, it - 1)
                    k_turn(it, u)
                    pe.wait_ge(qs0_done, it + 1)
                    q_turn(it, u, 1)
                if there(b4_):
                    pe.wait_ge(onts_done, b4_ + 1)
                    for j in range(DH):
                        last = mm(P_PJ[:, D:2 * D], ONT[:, j, :], WCT[:, j, :], start=(j == 0), stop=(j == DH - 1))
                    last.then_inc(proj_done, 1)
                if there(b1_):
                    pe.wait_ge(qs1_done, b1_ + 1)
                    for g in (2, 3):
                        scores_max(b1_, r1, g)
                if there(b3_):
                    pe.wait_ge(exp_done, G * (b3_ + 1))
                    pe.wait_ge(v1_done, b3_ + 2)
                    wait(pe, on_done, b3_)
                    for g in range(G):
                        last = mm(P_AT[32 * g:32 * (g + 1), :], V1[:, r3 % 2, g, :], PR[:, r3 % 2, g, :],
                                  start=True, stop=True, tile_position=(0, 32 * g))
                    last.then_inc(at_done, 1)
                if static(it) and it in (NB + 2, NB + 3):
                    weights(it - NB - 2)

            def weights(w):
                pe.wait_ge(wq_done, w + 1)
                for j in range(2):
                    wait(pe, wts_done, 2 * w + j - 1)
                    if w == 0:
                        pe.wait_ge(max_done, HG * NB)
                    for m in range(NF):
                        if w == 0:
                            src = W1Q[:, m, j * 128:(j + 1) * 128]
                        else:
                            f, dh = j * NF // 2 + m // DH, m % DH
                            src = W2Q[:, dh, f * 128:(f + 1) * 128]
                        last = tr(as_bf16(P_MAX[j])[:, m * 128:(m + 1) * 128], src, IDB[:, :])
                    last.then_inc(wt_done, 1)
            pipeline(pe, step)

            def turn(n):
                pe.wait_ge(y_done, BG * (n + 1))
                wait(pe, yts_done, n)
                for j in range(DH):
                    for s in range(BG):
                        last = tr(as_bf16(P_YT)[:, (j * BG + s) * S:(j * BG + s + 1) * S],
                                  Y[:, n * BG + s, j * 128:(j + 1) * 128], IDB[:, :])
                last.then_inc(yt_done, 1)

            def hidden(n, f):
                i = n * NF + f
                wait(pe, relu_done, i - 2)
                for j in range(DH):
                    last = mm(P_H[i % 3][:, :], W1T[:, j, f * 128:(f + 1) * 128], YT[:, n % 2, j, :],
                              start=(j == 0), stop=(j == DH - 1))
                last.then_inc(h_done, 1)

            def output(n, s):
                b = n * BG + s
                wait(pe, res_done, b - 1)
                for f in range(NF):
                    if s == 0:
                        pe.wait_ge(hq_done, n * NF + f + 1)
                    last = mm(P_O[s % 2][:, 0:D], HQ[:, n % 2, f, s * S:(s + 1) * S], W2T[:, f, :],
                              start=(f == 0), stop=(f == NF - 1))
                last.then_inc(o_done, 1)

            pe.wait_ge(qs1_done, NB)
            turn(0)
            pe.wait_ge(wts_done, 4)
            pe.wait_ge(exp_done, G * NB)
            pe.wait_ge(x1_done, NB)
            for n in range(NG + 1):
                if n < NG:
                    pe.wait_ge(yts_done, n + 1)
                for f in range(NF):
                    if n < NG:
                        hidden(n, f)
                    if f == 2 and n + 1 < NG:
                        turn(n + 1)
                    if n >= 1 and f % 2 == 1:
                        output(n - 1, f // 2)

    return nc


_INS = ['x', 'ctx_512', 'L0_xattn_Wc', 'L0_xattn_bc', 'L0_ffn_W1', 'L0_ffn_b1', 'L0_ffn_W2', 'L0_ffn_b2',
        'L0_ffn_s_act1', 'L0_ffn_s_act2']


def kernel(**inputs):
    import numpy as _np
    import concourse.bacc as _bacc
    from concourse import mybir as _mybir
    from concourse.bass_utils import run_bass_kernel_spmd as _run

    nc = _bacc.Bacc("TRN2", target_bir_lowering=False, num_devices=1)
    arrays, args = {}, []
    for name in _INS:
        a = _np.ascontiguousarray(inputs[name])
        arrays[f"in_{name}"] = a
        args.append(nc.dram_tensor(f"in_{name}", a.shape, _mybir.dt.from_np(a.dtype), kind="ExternalInput").ap())
    out = nc.dram_tensor("out_x", inputs['x'].shape, _mybir.dt.float32, kind="ExternalOutput").ap()
    xattn_ffn(nc, *args, out)
    r = _run(nc, [arrays], core_ids=[0])
    return r.results[0]["out_x"]
```

```python
import concourse.bass as bass
from concourse import mybir
from contextlib import ExitStack


def xattn_ffn(nc, x, ctx_512, Wc, bc, W1, b1, W2, b2, s_act1, s_act2, out):
    f32, bf16 = mybir.dt.float32, mybir.dt.bfloat16
    RMAX = bass.bass_isa.ReduceOp.max
    ALU, ACT, AX = mybir.AluOpType, mybir.ActivationFunctionType, mybir.AxisListType

    NB, S, D = x.shape
    DK = ctx_512.shape[2]
    F = W1.shape[0]
    H, G = 16, 4
    HD = D // H
    HG = H // G
    NH = H + G
    W = D + DK
    COMBO = 6
    KR = COMBO * HD
    KM = KR + 2
    DH = D // 128
    NF = F // 128
    AR = 3
    RING = 4
    LAST = 4
    NG = 4
    BG = NB // NG
    TG = BG * S
    EPS = 1e-5
    MAGIC = 1.5 * 2.0 ** 23
    QMAX, QMIN, UMAX = 7.0, -8.0, 15.0
    IMAX = 2.0 ** 22

    es = ExitStack()
    with es:
        def sb(name, shape, dt):
            return es.enter_context(nc.sbuf_tensor(name, shape, dt))

        def sem(name):
            return es.enter_context(nc.semaphore(name))

        X = sb("X", [S, NB, D], f32)
        QK = sb("QK", [S, NB + 1, W], f32)
        X1 = sb("X1", [S, NB, D], f32)
        Y = sb("Y", [S, NB, D], bf16)
        PARTS = sb("PARTS", [S, 2, NH, COMBO, HD], bf16)
        REST = sb("REST", [S, 2, W], f32)
        QS = sb("QS", [KM, RING, H, S], bf16)
        KS = sb("KS", [KM, RING, G, S], bf16)
        NMAX = sb("NMAX", [S, 2, H], f32)
        NMP = sb("NMP", [S, 2, 2 * H], bf16)
        NMT = sb("NMT", [2 * H, 2, S], bf16)
        V1 = sb("V1", [S, 2, G, 32], f32)
        PR = sb("PR", [S, 2, G, HG * S], f32)
        OT = sb("OT", [128, HG * S], f32)
        RSUM = sb("RSUM", [S, H], f32)
        ON = sb("ON", [S, G, HG, HD], f32)
        ONT = sb("ONT", [128, DH, S], f32)
        ST1 = sb("ST1", [S, NB, 6], f32)
        MV1 = sb("MV1", [S, NB, 2], f32)
        RS1 = sb("RS1", [S, NB], f32)
        NM1 = sb("NM1", [S, NB], f32)
        VE1 = sb("VE1", [S, NB], f32)
        ST2 = sb("ST2", [S, RING, 6], f32)
        MV2 = sb("MV2", [S, RING, 2], f32)
        VE2 = sb("VE2", [S, RING], f32)
        RS2 = sb("RS2", [S, RING], f32)
        RQ2 = sb("RQ2", [S, RING], f32)
        YA = sb("YA", [S, 2, D], f32)
        YB = sb("YB", [S, 2, D], f32)
        HALF = sb("HALF", [S, NB], f32)
        IDF = sb("IDF", [128, 128], f32)
        IDB = sb("IDB", [128, 128], bf16)
        MAG = sb("MAG", [128, 1], f32)
        BC = sb("BC", [S, D], f32)
        B12 = sb("B12", [128, NF + D], f32)
        SA = sb("SA", [128, 2], f32)
        SC = sb("SC", [128, 16], f32)
        WCR = sb("WCR", [128, DH, D], f32)
        WCT = sb("WCT", [128, DH, D], f32)
        W1R = sb("W1R", [128, NF, D], f32)
        W2R = sb("W2R", [128, DH, F], f32)
        W1Q = sb("W1Q", [128, NF, D], bf16)
        W2Q = sb("W2Q", [128, DH, F], bf16)
        W1T = sb("W1T", [128, DH, F], bf16)
        W2T = sb("W2T", [128, NF, D], bf16)
        YT = sb("YT", [128, 2, DH, TG], bf16)
        HF = sb("HF", [128, 2, TG], f32)
        HM = sb("HM", [128, 2, TG], f32)
        HQ = sb("HQ", [128, 2, NF, TG], bf16)
        OUT = sb("OUT", [S, 2, BG, D], f32)
        TB = sb("TB", [128, NF + D], f32)
        AMAX = sb("AMAX", [128, 2], f32)
        EPST = sb("EPST", [128, 1], f32)
        WARM = sb("WARM", [128, 1], f32)

        def bank(name):
            return es.enter_context(nc.psum_tensor(name, [128, 512], f32))
        P_MAX = [bank("P_MAX0"), bank("P_MAX1")]
        P_EXP = [bank("P_EXP0"), bank("P_EXP1")]
        P_QT = bank("P_QT")
        P_KT = bank("P_KT")
        P_AT = bank("P_AT")
        P_PJ = bank("P_PJ")

        P_W = [P_MAX[0], P_MAX[1], P_QT, P_KT]
        P_H = [P_MAX[0], P_MAX[1], P_KT]
        P_O = [P_AT, P_PJ]
        P_YT = P_QT

        def as_bf16(t):
            return t[:, :].bitcast(bf16)

        x_in = [sem(f"x_in{c}") for c in range(5)]
        ctx_in = [sem(f"ctx_in{c}") for c in range(2)]
        bc_in, wc_in, w1_in, w2_in, sa_in, bias_in = (sem(n) for n in ("bc_in", "wc_in", "w1_in", "w2_in", "sa_in", "bias_in"))
        zeroed, consts_ready = sem("zeroed"), sem("consts_ready")
        ones_done = sem("ones_done")
        st1_done, mv1_done, ve1_done, rs1_done, q_done = (sem(n) for n in ("st1_done", "mv1_done", "ve1_done", "rs1_done", "q_done"))
        part1_done, rest_done, part2_done, part3_done = (sem(n) for n in ("part1_done", "rest_done", "part2_done", "part3_done"))
        nm1_done = sem("nm1_done")
        xb_done, v1_done = sem("xb_done"), sem("v1_done")
        qt_done, qs0_done, qs1_done = sem("qt_done"), sem("qs0_done"), sem("qs1_done")
        kt_done, ks_done = sem("kt_done"), sem("ks_done")
        smax_done, max_done, nmp1_done, nmp2_done = sem("smax_done"), sem("max_done"), sem("nmp1_done"), sem("nmp2_done")
        nmt_done, nmts_done = sem("nmt_done"), sem("nmts_done")
        nm_row = [sem("nm_row0"), sem("nm_row1")]
        sexp_done, exp_done, at_done, ats_done = sem("sexp_done"), sem("exp_done"), sem("at_done"), sem("ats_done")
        back_done, rsum_done, on_done, ont_done, onts_done = (sem(n) for n in ("back_done", "rsum_done", "on_done", "ont_done", "onts_done"))
        proj_done, x1_done, st2_done, mv2_done = sem("proj_done"), sem("x1_done"), sem("st2_done"), sem("mv2_done")
        ve2_done, rs2_done, rq2_done = sem("ve2_done"), sem("rs2_done"), sem("rq2_done")
        ya_done, yb_done, y_done = sem("ya_done"), sem("yb_done"), sem("y_done")
        wct_done, wcts_done = sem("wct_done"), sem("wcts_done")
        amax_done, amaxall_done, scales = sem("amax_done"), sem("amaxall_done"), sem("scales")
        wm_done, wq_done, wt_done, wts_done = sem("wm_done"), sem("wq_done"), sem("wt_done"), sem("wts_done")
        x1b_done, warm_done = sem("x1b_done"), sem("warm_done")
        yt_done, yts_done, h_done, relu_done, hm_done, hq_done = (sem(n) for n in ("yt_done", "yts_done", "h_done", "relu_done", "hm_done", "hq_done"))
        o_done, res_done = sem("o_done"), sem("res_done")
        out_sent = [sem("out_sent0"), sem("out_sent1")]

        AHEAD = {NB + 2: ((), (), (0, 1)), NB + 3: ((2, 3), (4, 5), (6, 7))}
        NORMS = {1: (4,), 2: (5,), 3: (6, 7), 4: (8, 9), 5: (10, 11), 6: (12, 13), 7: (14, 15)}
        CH = [(0, 1), (1, 4), (4, 8), (8, 12), (12, 16)]
        CC = [(0, 4), (4, 16)]
        AMX, RMX, SW, SS, RSS, CH_, RSA1, RSA2 = 0, 2, 4, 6, 8, 10, 11, 12

        QH, KH = slice(0, H), slice(H, NH)
        QSLOTS = {1: (QH, slice(0, 3)), 2: (QH, slice(3, 5)), 3: (QH, slice(5, 6))}
        KSLOTS = {1: (KH, slice(1, 6, 2)), 2: (KH, slice(0, 5, 4)), 3: (KH, slice(2, 3))}

        def static(b):
            return isinstance(b, int)

        def there(b, first=0, last=NB - 1):
            return not static(b) or first <= b <= last

        def wait(eng, s, value):
            if not static(value) or value > 0:
                eng.wait_ge(s, value)

        def pipeline(eng, step, head=None, first=RING, last=LAST):
            head = head or (lambda it, u: None)
            for it in range(first):
                head(it, it % RING)
                step(it, it % RING)
            head(first, 0)
            with eng.Fori(first // RING, NB // RING) as k:
                for u in range(RING):
                    step(k * RING + u, u)
                    head(k * RING + u + 1, (u + 1) % RING)
            for it in range(NB, NB + last):
                step(it, it % RING)
                head(it + 1, (it + 1) % RING)

        def nm_rows(it, u, lag):
            return (it - u) * 8 + 16 * ((u - lag) // 2 + 1)

        block = es.enter_context(nc.Block())

        @block.sync
        def _(sp):
            def load_x(c):
                a, b = CH[c]
                sp.dma_start(X[:, a:b, :], x[a:b].rearrange("b s d -> s b d")).then_inc(x_in[c], 16)

            def load_ctx(c):
                a, b = CC[c]
                sp.dma_start(QK[:, a:b, D:W], ctx_512[a:b].rearrange("b s d -> s b d")).then_inc(ctx_in[c], 16)
            load_x(0)
            load_ctx(0)
            load_x(1)
            load_x(2)
            sp.dma_start(W1R[:, :, :], W1.rearrange("(j p) k -> p j k", p=128)).then_inc(w1_in, 16)
            sp.dma_start(BC[:, :], bc.rearrange("(a n) -> a n", a=1).to_broadcast([S, D])).then_inc(bc_in, 16)
            sp.dma_start(SA[:, 0:1], s_act1.rearrange("(a n) -> a n", a=1).to_broadcast([128, 1])).then_inc(sa_in, 16)
            sp.dma_start(SA[:, 1:2], s_act2.rearrange("(a n) -> a n", a=1).to_broadcast([128, 1])).then_inc(sa_in, 16)
            load_x(3)
            sp.dma_start(W2R[:, :, :], W2.rearrange("(j p) k -> p j k", p=128)).then_inc(w2_in, 16)
            load_ctx(1)
            load_x(4)
            sp.dma_start(WCR[:, :, :], Wc.rearrange("(j p) k -> p j k", p=128)).then_inc(wc_in, 16)
            sp.dma_start(B12[:, NF:], b2.rearrange("(a n) -> a n", a=1).to_broadcast([S, D])).then_inc(bias_in, 16)
            with nc.allow_non_contiguous_dma(reason="1024 biases, one to a partition and tile"):
                sp.dma_start(B12[:, 0:NF], b1.rearrange("(j p) -> p j", p=128)).then_inc(bias_in, 16)

            def step(it, u):
                b, r = it - 2, (u - 2) % RING
                if there(b):
                    sp.wait_ge(nmts_done, b + 1)
                    sp.dma_start(QS[KR:KM, r, :, :], NMT[:, r % 2, :]).then_inc(nm_row[r % 2], 16)
            pipeline(sp, step)

            for n in range(NG):
                sp.wait_ge(res_done, BG * (n + 1))
                sp.dma_start(out[n * BG:(n + 1) * BG].rearrange("b s d -> s b d"),
                             OUT[:, n % 2, :, :]).then_inc(out_sent[n % 2], 16)
            sp.wait_ge(out_sent[0], 16 * (NG // 2))
            sp.wait_ge(out_sent[1], 16 * (NG // 2))

        @block.gpsimd
        def _(pool):
            pool.memset(HALF[:, :], -0.5).then_inc(zeroed, 1)
            pool.memset(EPST[:, :], EPS).then_inc(zeroed, 1)
            pool.memset(IDF[:, :], 0.0).then_inc(zeroed, 1)
            pool.memset(IDB[:, :], 0.0).then_inc(zeroed, 1)
            pool.memset(MAG[:, :], MAGIC).then_inc(consts_ready, 1)
            pool.wait_ge(zeroed, 4)
            for t in (IDF, IDB):
                pool.affine_select(out=t[:, :], in_=t[:, :], compare_op=ALU.not_equal, fill=1.0, base=0,
                                   pattern=[[-1, 128]], channel_multiplier=1).then_inc(consts_ready, 1)

            def rstd1(c):
                a, b = CH[c]
                pool.wait_ge(mv1_done, b)
                pool.tensor_scalar(VE1[:, a:b], MV1[:, a:b, 1], EPS, float(HD), ALU.add, ALU.mult).then_inc(ve1_done, 1)
                pool.wait_ge(ve1_done, c + 1)
                pool.tensor_tensor(RS1[:, a:b], VE1[:, a:b], HALF[:, a:b], ALU.pow).then_inc(rs1_done, 1)
                if c >= 2:
                    pool.tensor_scalar(NM1[:, a:b], MV1[:, a:b, 0], -1.0, 0.0, ALU.mult, ALU.add).then_inc(nm1_done, 1)
                    pool.wait_ge(nm1_done, c - 1)
                    pool.wait_ge(rs1_done, c + 1)

            def norm1(batches):
                for i in batches:
                    pool.wait_ge(q_done, i)
                    pool.tensor_scalar(QK[:, i, 0:D], X[:, i, :], NM1[:, i:i + 1], RS1[:, i:i + 1],
                                       ALU.add, ALU.mult).then_inc(q_done, 1)
                if batches[-1] == NB - 1:
                    pool.wait_ge(q_done, NB)
                    pool.memset(QK[:, NB, :], 0.0).then_inc(q_done, 1)

            rstd1(0)
            pool.memset(V1[:, :, :, HD:32], 0.0).then_inc(zeroed, 1)
            pool.wait_ge(zeroed, 5)
            pool.memset(V1[:, :, :, HD:HD + 1], 1.0).then_inc(v1_done, 1)

            def rest(b, r):
                pool.wait_ge(part1_done, 2 * (b + 1))
                wait(pool, part3_done, 2 * (b - 1))
                pool.tensor_tensor(REST[:, r % 2, :].rearrange("p (h d) -> p h d", d=HD),
                                   QK[:, b, :].rearrange("p (h d) -> p h d", d=HD),
                                   PARTS[:, r % 2, :, 1, :], ALU.subtract).then_inc(rest_done, 1)

            def part3(b, r):
                pool.wait_ge(part2_done, 2 * (b + 1))
                rest_ = REST[:, r % 2, :].rearrange("p (h d) -> p h d", d=HD)
                for hs, slot in QSLOTS[3], KSLOTS[3]:
                    pool.tensor_tensor(PARTS[:, r % 2, hs, slot, :], rest_[:, hs, :].unsqueeze(2), PARTS[:, r % 2, hs, 4:5, :],
                                       ALU.subtract).then_inc(part3_done, 1)

            rest(0, 0)
            rstd1(1)
            part3(0, 0)
            rstd1(2)
            pool.wait_ge(bc_in, 16)

            def step(it, u):
                if there(it + 1, 0, NB):
                    rest(it + 1, (u + 1) % RING)
                if there(it):
                    pool.wait_ge(q_done, it + 1)
                    pool.tensor_tensor(X[:, it, :], X[:, it, :], BC[:, :], ALU.add).then_inc(xb_done, 1)
                if there(it - 5):
                    b, r = it - 5, (u - 5) % RING
                    pool.wait_ge(mv2_done, b + 1)
                    pool.tensor_tensor(VE2[:, r:r + 1], MV2[:, r, 1:2], EPST[:, :], ALU.add).then_inc(ve2_done, 1)
                    pool.wait_ge(ve2_done, b + 1)
                    pool.tensor_tensor(RS2[:, r:r + 1], VE2[:, r:r + 1], HALF[:, 0:1], ALU.pow).then_inc(rs2_done, 1)
                    if static(b) and b == 0:
                        pool.wait_ge(scales, 1)
                    pool.wait_ge(rs2_done, b + 1)
                    pool.tensor_tensor(RQ2[:, r:r + 1], RS2[:, r:r + 1], SC[:, RSA1:RSA1 + 1], ALU.mult).then_inc(rq2_done, 1)
                if there(it - 2):
                    b, r = it - 2, (u - 2) % RING
                    wait(pool, at_done, b - 1)
                    pool.wait_ge(ctx_in[0 if static(b) and b < CC[0][1] else 1], 16)
                    pool.tensor_copy(V1[:, r % 2, :, 0:HD],
                                     QK[:, b, D:W].rearrange("p (g d) -> p g d", g=G)).then_inc(v1_done, 1)
                if there(it + 1, 0, NB):
                    part3(it + 1, (u + 1) % RING)
                if static(it) and it in (2, 4):
                    rstd1(it // 2 + 2)
                if static(it) and it in NORMS:
                    norm1(NORMS[it])
                if static(it) and it == AR:
                    pool.wait_ge(amax_done, 2)
                    pool.partition_all_reduce(AMAX[:, :], SC[:, AMX:AMX + 2], 128, RMAX).then_inc(amaxall_done, 2)
            pipeline(pool, step, first=2 * RING, last=LAST + 1)
            pool.wait_ge(scales, 16)
            for b in range(NB):
                pool.wait_ge(y_done, b + 1)
                pool.tensor_tensor(X1[:, b, :], X1[:, b, :], B12[:, NF:], ALU.add).then_inc(x1b_done, 1)

        @block.vector
        def _(dve):
            vec = nc.vector
            vec.memset(KS[KR:KM, :, :, :], 1.0).then_inc(ones_done, 1)

            def stats1(a, b):
                for c, (first, _) in enumerate(CH):
                    if first in range(a, b):
                        dve.wait_ge(x_in[c], 16)
                for i in range(a, b):
                    vec.bn_stats(ST1[:, i, :], X[:, i, :]).then_inc(st1_done, 1)
                for i in range(a, b):
                    dve.wait_ge(st1_done, i + 1)
                    vec.bn_aggr(MV1[:, i, :], ST1[:, i, :]).then_inc(mv1_done, 1)

            def norm1(c):
                a, b = CH[c]
                dve.wait_ge(rs1_done, c + 1)
                for i in range(a, b):
                    vec.tensor_scalar(QK[:, i, 0:D], X[:, i, :], MV1[:, i, 0:1], RS1[:, i:i + 1],
                                      ALU.subtract, ALU.mult).then_inc(q_done, 1)

            def small(ins, n):
                ins.then_inc(scales, 1)
                dve.wait_ge(scales, n)

            def abs_max(w):
                dve.wait_ge((w1_in, w2_in)[w], 16)
                vec.tensor_reduce(SC[:, AMX + w:AMX + w + 1], (W1R, W2R)[w][:, :, :], AX.XY, ALU.max,
                                  apply_absolute_value=True).then_inc(amax_done, 1)

            stats1(*CH[0])
            norm1(0)
            stats1(*CH[1])
            norm1(1)
            stats1(*CH[2])
            dve.wait_ge(sa_in, 32)
            small(vec.reciprocal(SC[:, RSA1:RSA1 + 2], SA[:, 0:2]), 1)

            def row_max(b, r, g):
                i = b * HG + g
                dve.wait_ge(smax_done, i + 1)
                if g == 0:
                    wait(dve, nmp2_done, b - 1)
                vec.tensor_reduce(NMAX[:, r % 2, g * HG:(g + 1) * HG],
                                  P_MAX[g % 2][:, :].rearrange("p (h t) -> p h t", t=S),
                                  AX.X, ALU.max, negate=True).then_inc(max_done, 1)

            def head(it, u):
                late = there(it - 5)
                b5, r5 = it - 5, (u - 5) % RING
                if late:
                    dve.wait_ge(proj_done, b5 + 1)
                    dve.wait_ge(xb_done, b5 + 1)
                    vec.tensor_tensor(X1[:, b5, :], P_PJ[:, D:2 * D], X[:, b5, :], ALU.add).then_inc(x1_done, 1)
                    dve.wait_ge(x1_done, b5 + 1)
                if there(it - 4):
                    b = it - 4
                    dve.wait_ge(back_done, b + 1)
                    back = P_AT[:, :].rearrange("p (h g e) -> p h g e", h=HG, g=G)
                    vec.reciprocal(RSUM[:, :].rearrange("p (h g) -> p h g", h=HG), back[:, :, :, HD]).then_inc(rsum_done, 1)
                    if late:
                        vec.bn_stats(ST2[:, r5, :], X1[:, b5, :]).then_inc(st2_done, 1)
                    dve.wait_ge(rsum_done, b + 1)
                    wait(dve, ont_done, b)
                    vec.tensor_tensor(ON[:, :, :, :].rearrange("p g h d -> p h g d"), back[:, :, :, 0:HD],
                                      RSUM[:, :].rearrange("p (h g) -> p h g", h=HG).unsqueeze(3).to_broadcast([S, HG, G, HD]),
                                      ALU.mult).then_inc(on_done, 1)
                if late and not there(it - 4):
                    vec.bn_stats(ST2[:, r5, :], X1[:, b5, :]).then_inc(st2_done, 1)
                if late:
                    dve.wait_ge(st2_done, b5 + 1)
                if there(it - 2):
                    b2_, r2 = it - 2, (u - 2) % RING
                    dve.wait_ge(nmp1_done, b2_ + 1)
                    vec.tensor_tensor(NMP[:, r2 % 2, H:2 * H], NMAX[:, r2 % 2, :], NMP[:, r2 % 2, 0:H],
                                      ALU.subtract).then_inc(nmp2_done, 1)
                if there(it - 1):
                    row_max(it - 1, (u - 1) % RING, 0)
                if late:
                    vec.bn_aggr(MV2[:, r5, :], ST2[:, r5, :]).then_inc(mv2_done, 1)
                if there(it - 1):
                    row_max(it - 1, (u - 1) % RING, 1)

            def step(it, u):
                r = u % RING
                b1_, r1 = it - 1, (u - 1) % RING
                if static(it):
                    extra(it)
                if there(b1_):
                    row_max(b1_, r1, 2)
                    row_max(b1_, r1, 3)
                    dve.wait_ge(max_done, HG * (b1_ + 1))
                    wait(dve, nmt_done, b1_ - 1)
                    vec.tensor_copy(NMP[:, r1 % 2, 0:H], NMAX[:, r1 % 2, :]).then_inc(nmp1_done, 1)
                b5, r5 = it - 5, (u - 5) % RING
                if there(b5):
                    dve.wait_ge(rq2_done, b5 + 1)
                    wait(dve, yb_done, b5)
                    vec.tensor_scalar(YA[:, r5 % 2, :], X1[:, b5, :], MV2[:, r5, 0:1], RQ2[:, r5:r5 + 1],
                                      ALU.subtract, ALU.mult).then_inc(ya_done, 1)
                if there(it):
                    dve.wait_ge(qt_done, 2 * it + 2)
                    wait(dve, sexp_done, G * (it - RING + 1))
                    vec.tensor_copy(QS[0:KR, r, H // 2:H, :],
                                    as_bf16(P_QT)[0:KR, :].rearrange("p (h s) -> p h s", s=S)).then_inc(qs1_done, 1)
                if there(b5):
                    dve.wait_ge(ya_done, b5 + 1)
                    wait(dve, y_done, b5)
                    vec.tensor_scalar(YB[:, r5 % 2, :], YA[:, r5 % 2, :], QMAX, QMIN, ALU.min, ALU.max).then_inc(yb_done, 1)
                    dve.wait_ge(yb_done, b5 + 1)
                    vec.tensor_scalar(Y[:, b5, :], YB[:, r5 % 2, :], MAGIC, MAGIC, ALU.add, ALU.subtract).then_inc(y_done, 1)
                ahead(it)

            def extra(it):
                if it == 1:
                    abs_max(0)
                if it == 2:
                    abs_max(1)
                    dve.wait_ge(wct_done, 1)
                    vec.tensor_copy(WCT[:, :, :], P_PJ[:, :].rearrange("p (j n) -> p j n", j=DH)).then_inc(wcts_done, 1)
                if it == 3:
                    stats1(*CH[3])
                if it == 4:
                    inverse_scales()
                    stats1(*CH[4])
                if it == 6:
                    w_int(0)
                if it == NB + 1:
                    w_out(0)
                    scales_and_biases()
                    w_int(1)
                if it == NB + 3:
                    w_out(1)

            def ahead(it):
                if static(it):
                    for f in sum(AHEAD.get(it, ()), ()):
                        quantise(0, f)

            def w_int(w):
                dve.wait_ge(wm_done, w + 1)
                src, dst = ((W1R, W1Q), (W2R, W2Q))[w]
                vec.tensor_scalar(dst[:, :, :], src[:, :, :], MAGIC, 1.0, ALU.subtract, ALU.mult).then_inc(wq_done, 1)

            def w_out(w):
                for j in range(2):
                    i = 2 * w + j
                    dve.wait_ge(wt_done, i + 1)
                    src = as_bf16(P_W[i])[:, :]
                    if w == 0:
                        vec.tensor_copy(W1T[:, j, :], src).then_inc(wts_done, 1)
                    else:
                        vec.tensor_copy(W2T[:, j * NF // 2:(j + 1) * NF // 2, :],
                                        src.rearrange("p (f k) -> p f k", k=D)).then_inc(wts_done, 1)

            def inverse_scales():
                dve.wait_ge(amaxall_done, 2)
                small(vec.reciprocal(SC[:, RMX:RMX + 2], AMAX[:, :]), 2)
                small(vec.tensor_scalar(SC[:, RMX:RMX + 2], SC[:, RMX:RMX + 2], QMAX, 1.0, ALU.mult, ALU.mult), 3)

            def scales_and_biases():
                small(vec.tensor_scalar(SC[:, SW:SW + 2], AMAX[:, :], 1.0 / QMAX, 1.0, ALU.mult, ALU.mult), 4)
                small(vec.tensor_tensor(SC[:, SS:SS + 2], SA[:, :], SC[:, SW:SW + 2], ALU.mult), 5)
                vec.tensor_tensor(SC[:, CH_:CH_ + 1], SC[:, SS:SS + 1], SC[:, RSA2:RSA2 + 1], ALU.mult).then_inc(scales, 1)
                small(vec.reciprocal(SC[:, RSS:RSS + 2], SC[:, SS:SS + 2]), 7)
                dve.wait_ge(bias_in, 32)
                vec.tensor_scalar(B12[:, 0:NF], B12[:, 0:NF], SC[:, RSS:RSS + 1], 1.0, ALU.mult, ALU.mult).then_inc(scales, 1)
                small(vec.tensor_scalar(B12[:, NF:], B12[:, NF:], SC[:, RSS + 1:RSS + 2], 1.0, ALU.mult, ALU.mult), 9)
                small(vec.tensor_scalar(TB[:, :], B12[:, :], IMAX, -IMAX, ALU.min, ALU.max), 10)
                small(vec.tensor_tensor(B12[:, :], B12[:, :], TB[:, :], ALU.subtract), 11)
                small(vec.tensor_scalar(TB[:, :], TB[:, :], MAGIC, MAGIC, ALU.add, ALU.subtract), 12)
                small(vec.tensor_tensor(B12[:, :], B12[:, :], TB[:, :], ALU.add), 13)
                small(vec.tensor_scalar(B12[:, :], B12[:, :], 2.0 ** 31, -2.0 ** 31, ALU.min, ALU.max), 14)
                vec.tensor_scalar(B12[:, 0:NF], B12[:, 0:NF], SC[:, CH_:CH_ + 1], 1.0, ALU.mult, ALU.mult).then_inc(scales, 1)
                vec.tensor_scalar(B12[:, NF:], B12[:, NF:], SC[:, SS + 1:SS + 2], 1.0, ALU.mult, ALU.mult).then_inc(scales, 1)

            def quantise(n, f):
                i = n * NF + f
                dve.wait_ge(relu_done, i + 1)
                wait(dve, hq_done, i - 1)
                vec.tensor_scalar(HM[:, i % 2, :], HF[:, i % 2, :], UMAX, MAGIC, ALU.min, ALU.add).then_inc(hm_done, 1)
                dve.wait_ge(hm_done, i + 1)
                if f == 0:
                    wait(dve, o_done, BG * (n - 1))
                vec.tensor_scalar(HQ[:, n % 2, f, :], HM[:, i % 2, :], MAGIC, 1.0, ALU.subtract, ALU.mult).then_inc(hq_done, 1)

            def result(n, s):
                b = n * BG + s
                dve.wait_ge(o_done, b + 1)
                dve.wait_ge(x1b_done, b + 1)
                if s == 0 and n >= 2:
                    dve.wait_ge(out_sent[n % 2], 16 * (n // 2))
                vec.scalar_tensor_tensor(out=OUT[:, n % 2, s, :], in0=P_O[s % 2][:, 0:D], scalar=SC[:, SS + 1:SS + 2],
                                         in1=X1[:, b, :], op0=ALU.mult, op1=ALU.add).then_inc(res_done, 1)

            pipeline(dve, step, head, first=2 * RING, last=LAST + 1)
            for n in range(NG + 1):
                for f in range(NF):
                    if (n or f > AHEAD[NB + LAST - 1][2][-1]) and n < NG:
                        quantise(n, f)
                    if n >= 1 and f % 2 == 1:
                        result(n - 1, f // 2)


        @block.scalar
        def _(act):
            sc = nc.scalar

            def part1(b, r):
                act.wait_ge(q_done, b + 1)
                act.wait_ge(ctx_in[0 if static(b) and b < CC[0][1] else 1], 16)
                wait(act, qt_done, 2 * (b - 1))
                wait(act, kt_done, b - 1)
                spread(QK[:, b, :], r, 1, part1_done)

            def spread(value, r, part, done):
                value = value.rearrange("p (h d) -> p h d", d=HD)
                for hs, slots in QSLOTS[part], KSLOTS[part]:
                    to = PARTS[:, r % 2, hs, slots, :]
                    sc.copy(to, value[:, hs, :].unsqueeze(2).to_broadcast(list(to.shape))).then_inc(done, 1)

            def part2(b, r):
                act.wait_ge(rest_done, b + 1)
                spread(REST[:, r % 2, :], r, 2, part2_done)

            def exps(b, r, gs):
                for g in gs:
                    act.wait_ge(sexp_done, G * b + g + 1)
                    if g == 0:
                        wait(act, at_done, b - 1)
                    sc.activation(PR[:, r % 2, g, :], P_EXP[g % 2][:, :], ACT.Exp).then_inc(exp_done, 1)

            act.wait_ge(consts_ready, 1)
            sc.activation(WARM[:, :], MAG[:, :], ACT.Exp, scale=0.0).then_inc(warm_done, 1)
            part1(0, 0)
            part2(0, 0)

            def step(it, u):
                if there(it - 4):
                    b = it - 4
                    act.wait_ge(at_done, b + 1)
                    wait(act, back_done, b)
                    sc.copy(OT[:, :], P_AT[:, :]).then_inc(ats_done, 1)
                if there(it - 3):
                    exps(it - 3, (u - 3) % RING, (0, 1))
                if there(it + 1, 0, NB):
                    part1(it + 1, (u + 1) % RING)
                ahead(it, 0)
                if there(it - 3):
                    exps(it - 3, (u - 3) % RING, (2, 3))
                if there(it - 2):
                    b, r = it - 2, (u - 2) % RING
                    act.wait_ge(nmt_done, b + 1)
                    wait(act, nm_row[r % 2], nm_rows(it, u, 4))
                    sc.copy(NMT[:, r % 2, :], as_bf16(P_KT)[0:2 * H, 0:S]).then_inc(nmts_done, 1)
                if there(it):
                    r = u % RING
                    act.wait_ge(qt_done, 2 * it + 1)
                    wait(act, sexp_done, G * (it - RING + 1))
                    sc.copy(QS[0:KR, r, 0:H // 2, :],
                            as_bf16(P_QT)[0:KR, :].rearrange("p (h s) -> p h s", s=S)).then_inc(qs0_done, 1)
                ahead(it, 1)
                if there(it - 4):
                    b = it - 4
                    act.wait_ge(ont_done, b + 1)
                    wait(act, proj_done, b)
                    sc.copy(ONT[:, :, :], P_PJ[:, 0:D].rearrange("p (j s) -> p j s", j=DH)).then_inc(onts_done, 1)
                if there(it):
                    act.wait_ge(kt_done, it + 1)
                    wait(act, sexp_done, G * (it - RING + 1))
                    sc.copy(KS[0:KR, r, :, :], as_bf16(P_KT)[0:KR, 0:G * S].rearrange("p (g t) -> p g t", t=S)).then_inc(ks_done, 1)
                if there(it + 1, 0, NB):
                    part2(it + 1, (u + 1) % RING)
                if static(it) and it in (5, NB):
                    w = int(it == NB)
                    act.wait_ge(scales, 3)
                    t = (W1R, W2R)[w]
                    sc.activation(t[:, :, :], t[:, :, :], ACT.Identity, bias=MAG[:, 0:1],
                                  scale=SC[:, RMX + w:RMX + w + 1]).then_inc(wm_done, 1)
                if static(it) and it == NB:
                    turned(0)
                ahead(it, 2)

            def ahead(it, place):
                if static(it) and it in AHEAD:
                    for f in AHEAD[it][place]:
                        relu(0, f)

            def turned(n):
                act.wait_ge(yt_done, n + 1)
                wait(act, h_done, NF * (n - 1))
                sc.copy(YT[:, n % 2, :, :], as_bf16(P_YT)[:, :].rearrange("p (j s) -> p j s", j=DH)).then_inc(yts_done, 1)

            def relu(n, f):
                i = n * NF + f
                act.wait_ge(h_done, i + 1)
                if i == 0:
                    act.wait_ge(scales, 16)
                wait(act, hm_done, i - 1)
                sc.activation(HF[:, i % 2, :], P_H[i % 3][:, :], ACT.Relu, bias=B12[:, f:f + 1],
                              scale=SC[:, CH_:CH_ + 1]).then_inc(relu_done, 1)

            pipeline(act, step, first=2 * RING)
            for n in range(NG):
                for f in range(NF):
                    if n or f > AHEAD[NB + LAST - 1][2][-1]:
                        relu(n, f)
                    if f == 4 and n + 1 < NG:
                        turned(n + 1)

        @block.tensor
        def _(pe):
            mm, tr = nc.tensor.matmul, nc.tensor.transpose

            def q_turn(b, r, half):
                for j in range(H // 2):
                    last = tr(as_bf16(P_QT)[0:KR, j * S:(j + 1) * S],
                              PARTS[:, r % 2, half * (H // 2) + j, :, :].rearrange("p c d -> p (c d)"), IDB[:, :])
                last.then_inc(qt_done, 1)

            def k_turn(b, r):
                for g in range(G):
                    last = tr(as_bf16(P_KT)[0:KR, g * S:(g + 1) * S],
                              PARTS[:, r % 2, H + g, :, :].rearrange("p c d -> p (c d)"), IDB[:, :])
                last.then_inc(kt_done, 1)

            def scores_max(b, r, g):
                i = HG * b + g
                wait(pe, max_done, i - 1)
                for hh in range(HG):
                    last = mm(P_MAX[g % 2][:, hh * S:(hh + 1) * S], QS[0:KR, r, g * HG + hh, :], KS[0:KR, r, g, :],
                              start=True, stop=True)
                last.then_inc(smax_done, 1)

            def scores_exp(b, r, g):
                i = HG * b + g
                wait(pe, exp_done, i - 1)
                mm(P_EXP[g % 2][:, :], KS[:, r, g, :], QS[:, r, g * HG:(g + 1) * HG, :],
                   start=True, stop=True).then_inc(sexp_done, 1)

            pe.wait_ge(consts_ready, 3)

            def head(it, u):
                b3_, r3, b5_ = it - 3, (u - 3) % RING, it - 5
                if there(b3_):
                    if static(b3_) and b3_ == 0:
                        pe.wait_ge(ones_done, 1)
                    pe.wait_ge(nm_row[r3 % 2], nm_rows(it, u, 3))
                    for g in (0, 1):
                        scores_exp(b3_, r3, g)
                if there(b5_) and not (static(it) and it == LAST):
                    pe.wait_ge(onts_done, b5_ + 1)
                    for j in range(DH):
                        last = mm(P_PJ[:, D:2 * D], ONT[:, j, :], WCT[:, j, :], start=(j == 0), stop=(j == DH - 1))
                    last.then_inc(proj_done, 1)

            def step(it, u):
                b1_, b2_, b3_, b4_ = (it - l for l in (1, 2, 3, 4))
                r1, r2, r3, r4 = ((u - l) % RING for l in (1, 2, 3, 4))
                if there(b4_):
                    pe.wait_ge(ats_done, b4_ + 1)
                    for hh in range(HG):
                        last = tr(P_AT[:, hh * S:(hh + 1) * S], OT[:, hh * S:(hh + 1) * S], IDF[:, :])
                    last.then_inc(back_done, 1)
                ahead(it, 0)
                if there(b3_):
                    for g in (2, 3):
                        scores_exp(b3_, r3, g)
                if there(b1_):
                    pe.wait_ge(ks_done, b1_ + 1)
                    pe.wait_ge(qs0_done, b1_ + 1)
                    for g in (0, 1):
                        scores_max(b1_, r1, g)
                if there(b2_):
                    pe.wait_ge(nmp2_done, b2_ + 1)
                    wait(pe, ks_done, min(it, NB) if static(it) else it)
                    tr(as_bf16(P_KT)[0:2 * H, 0:S], NMP[:, r2 % 2, :], IDB[:, :]).then_inc(nmt_done, 1)
                if there(it):
                    pe.wait_ge(part3_done, 2 * (it + 1))
                    wait(pe, qs1_done, it)
                    q_turn(it, u, 0)
                if there(b4_):
                    pe.wait_ge(on_done, b4_ + 1)
                    wait(pe, x1_done, b4_)
                    if static(b4_) and b4_ == 0:
                        pe.wait_ge(wcts_done, 1)
                    on = ON[:, :, :, :].rearrange("p g h d -> p (g h d)")
                    for j in range(DH):
                        last = tr(P_PJ[:, j * S:(j + 1) * S], on[:, j * 128:(j + 1) * 128], IDF[:, :])
                    last.then_inc(ont_done, 1)
                ahead(it, 1)
                if there(it):
                    wait(pe, nmts_done, it - 1)
                    k_turn(it, u)
                if there(b1_):
                    pe.wait_ge(qs1_done, b1_ + 1)
                    for g in (2, 3):
                        scores_max(b1_, r1, g)
                if there(b3_):
                    pe.wait_ge(exp_done, G * (b3_ + 1))
                    pe.wait_ge(v1_done, b3_ + 2)
                    wait(pe, on_done, b3_)
                    for g in range(G):
                        last = mm(P_AT[32 * g:32 * (g + 1), :], V1[:, r3 % 2, g, :], PR[:, r3 % 2, g, :],
                                  start=True, stop=True, tile_position=(0, 32 * g))
                    last.then_inc(at_done, 1)
                if there(it):
                    pe.wait_ge(qs0_done, it + 1)
                    q_turn(it, u, 1)
                if static(it) and it == 1:
                    pe.wait_ge(wc_in, 16)
                    for j in range(DH):
                        for m in range(DH):
                            last = tr(P_PJ[:, j * D + m * 128:j * D + (m + 1) * 128],
                                      WCR[:, m, j * 128:(j + 1) * 128], IDF[:, :])
                    last.then_inc(wct_done, 1)
                if static(it) and it == NB:
                    turn(0)
                if static(it) and it in (NB, NB + 2):
                    weights(int(it != NB))
                ahead(it, 2)

            def ahead(it, place):
                if static(it) and it in AHEAD:
                    for f in AHEAD[it][place]:
                        hidden(0, f)

            def weights(w):
                pe.wait_ge(wq_done, w + 1)
                for j in range(2):
                    if w == 0:
                        pe.wait_ge(max_done, HG * NB)
                    else:
                        pe.wait_ge((yts_done, nmts_done)[j], (1, NB)[j])
                    for m in range(NF):
                        if w == 0:
                            src = W1Q[:, m, j * 128:(j + 1) * 128]
                        else:
                            f, dh = j * NF // 2 + m // DH, m % DH
                            src = W2Q[:, dh, f * 128:(f + 1) * 128]
                        last = tr(as_bf16(P_W[2 * w + j])[:, m * 128:(m + 1) * 128], src, IDB[:, :])
                    last.then_inc(wt_done, 1)

            def turn(n):
                pe.wait_ge(y_done, BG * (n + 1))
                wait(pe, yts_done, n)
                if n == 0:
                    pe.wait_ge(qs1_done, NB)
                if n == 1:
                    pe.wait_ge(wts_done, 4)
                for j in range(DH):
                    for s in range(BG):
                        last = tr(as_bf16(P_YT)[:, (j * BG + s) * S:(j * BG + s + 1) * S],
                                  Y[:, n * BG + s, j * 128:(j + 1) * 128], IDB[:, :])
                last.then_inc(yt_done, 1)

            def hidden(n, f):
                i = n * NF + f
                wait(pe, relu_done, i - 2)
                if i == 0:
                    pe.wait_ge(yts_done, 1)
                    pe.wait_ge(wts_done, 2)
                if i == 2:
                    pe.wait_ge(wts_done, 4)
                for j in range(DH):
                    last = mm(P_H[i % 3][:, :], W1T[:, j, f * 128:(f + 1) * 128], YT[:, n % 2, j, :],
                              start=(j == 0), stop=(j == DH - 1))
                last.then_inc(h_done, 1)

            def output(n, s):
                b = n * BG + s
                wait(pe, res_done, b - 1)
                for f in range(NF):
                    if s == 0:
                        pe.wait_ge(hq_done, n * NF + f + 1)
                    last = mm(P_O[s % 2][:, 0:D], HQ[:, n % 2, f, s * S:(s + 1) * S], W2T[:, f, :],
                              start=(f == 0), stop=(f == NF - 1))
                last.then_inc(o_done, 1)

            pipeline(pe, step, head)
            pe.wait_ge(x1_done, NB)
            for n in range(NG + 1):
                if n < NG:
                    pe.wait_ge(yts_done, n + 1)
                for f in range(NF):
                    if (n or f > AHEAD[NB + LAST - 1][2][-1]) and n < NG:
                        hidden(n, f)
                    if f == 2 and n + 1 < NG:
                        turn(n + 1)
                    if n >= 1 and f % 2 == 1:
                        output(n - 1, f // 2)

    return nc


_INS = ['x', 'ctx_512', 'L0_xattn_Wc', 'L0_xattn_bc', 'L0_ffn_W1', 'L0_ffn_b1', 'L0_ffn_W2', 'L0_ffn_b2',
        'L0_ffn_s_act1', 'L0_ffn_s_act2']


def kernel(**inputs):
    import numpy as _np
    import concourse.bacc as _bacc
    from concourse import mybir as _mybir
    from concourse.bass_utils import run_bass_kernel_spmd as _run

    nc = _bacc.Bacc("TRN2", target_bir_lowering=False, num_devices=1)
    arrays, args = {}, []
    for name in _INS:
        a = _np.ascontiguousarray(inputs[name])
        arrays[f"in_{name}"] = a
        args.append(nc.dram_tensor(f"in_{name}", a.shape, _mybir.dt.from_np(a.dtype), kind="ExternalInput").ap())
    out = nc.dram_tensor("out_x", inputs['x'].shape, _mybir.dt.float32, kind="ExternalOutput").ap()
    xattn_ffn(nc, *args, out)
    r = _run(nc, [arrays], core_ids=[0])
    return r.results[0]["out_x"]
```

```python
import concourse.bass as bass
from concourse import mybir
from contextlib import ExitStack


def xattn_ffn(nc, x, ctx_512, Wc, bc, W1, b1, W2, b2, s_act1, s_act2, out):
    f32, bf16 = mybir.dt.float32, mybir.dt.bfloat16
    RMAX = bass.bass_isa.ReduceOp.max
    ALU, ACT, AX = mybir.AluOpType, mybir.ActivationFunctionType, mybir.AxisListType

    NB, S, D = x.shape
    DK = ctx_512.shape[2]
    F = W1.shape[0]
    H, G = 16, 4
    HD = D // H
    HG = H // G
    NH = H + G
    W = D + DK
    COMBO = 6
    KR = COMBO * HD
    KM = KR + 2
    DH = D // 128
    NF = F // 128
    W1_STEP = 2
    RING = 4
    LAST = 4
    NG = 4
    BG = NB // NG
    TG = BG * S
    NT = NG * NF
    EPS = 1e-5
    MAGIC = 1.5 * 2.0 ** 23
    QMAX, QMIN, UMAX = 7.0, -8.0, 15.0
    IMAX = 2.0 ** 22

    es = ExitStack()
    with es:
        def sb(name, shape, dt):
            return es.enter_context(nc.sbuf_tensor(name, shape, dt))

        def sem(name):
            return es.enter_context(nc.semaphore(name))

        X = sb("X", [S, NB, D], f32)
        QK = sb("QK", [S, NB + 1, W], f32)
        X1 = sb("X1", [S, NB, D], f32)
        Y = sb("Y", [S, NB, D], bf16)
        PARTS = sb("PARTS", [S, 2, NH, COMBO, HD], bf16)
        REST = sb("REST", [S, 2, W], f32)
        QS = sb("QS", [KM, RING, H, S], bf16)
        KS = sb("KS", [KM, RING, G, S], bf16)
        NMAX = sb("NMAX", [S, 2, H], f32)
        NMP = sb("NMP", [S, 2, 2 * H], bf16)
        NMT = sb("NMT", [2 * H, 2, S], bf16)
        V1 = sb("V1", [S, 2, G, 32], f32)
        PR = sb("PR", [S, 2, G, HG * S], f32)
        OT = sb("OT", [128, HG * S], f32)
        RSUM = sb("RSUM", [S, H], f32)
        ON = sb("ON", [S, G, HG, HD], f32)
        ONT = sb("ONT", [128, DH, S], f32)
        ST1 = sb("ST1", [S, NB, 6], f32)
        MV1 = sb("MV1", [S, NB, 2], f32)
        RS1 = sb("RS1", [S, NB], f32)
        NM1 = sb("NM1", [S, NB], f32)
        VE1 = sb("VE1", [S, NB], f32)
        ST2 = sb("ST2", [S, RING, 6], f32)
        MV2 = sb("MV2", [S, RING, 2], f32)
        VE2 = sb("VE2", [S, RING], f32)
        RS2 = sb("RS2", [S, RING], f32)
        RQ2 = sb("RQ2", [S, RING], f32)
        YA = sb("YA", [S, 2, D], f32)
        YB = sb("YB", [S, 2, D], f32)
        HALF = sb("HALF", [S, NB], f32)
        IDF = sb("IDF", [128, 128], f32)
        IDB = sb("IDB", [128, 128], bf16)
        MAG = sb("MAG", [128, 1], f32)
        BC = sb("BC", [S, D], f32)
        B12 = sb("B12", [128, NF + D], f32)
        SA = sb("SA", [128, 2], f32)
        SC = sb("SC", [128, 16], f32)
        WCR = sb("WCR", [128, DH, D], f32)
        WCT = sb("WCT", [128, DH, D], f32)
        W1R = sb("W1R", [128, NF, D], f32)
        W2R = sb("W2R", [128, DH, F], f32)
        W1Q = sb("W1Q", [128, NF, D], bf16)
        W2Q = sb("W2Q", [128, DH, F], bf16)
        W1T = sb("W1T", [128, DH, F], bf16)
        W2T = sb("W2T", [128, NF, D], bf16)
        YT = sb("YT", [128, 2, DH, TG], bf16)
        HF = sb("HF", [128, 4, TG], f32)
        HM = sb("HM", [128, 4, TG], f32)
        HQ = sb("HQ", [128, 2, NF, TG], bf16)
        OUT = sb("OUT", [S, 2, BG, D], f32)
        TB = sb("TB", [128, NF + D], f32)
        AMAX = sb("AMAX", [128, 2], f32)
        EPST = sb("EPST", [128, 1], f32)
        WARM = sb("WARM", [128, 1], f32)

        def bank(name):
            return es.enter_context(nc.psum_tensor(name, [128, 512], f32))
        P_MAX = [bank("P_MAX0"), bank("P_MAX1")]
        P_EXP = [bank("P_EXP0"), bank("P_EXP1")]
        P_QT = bank("P_QT")
        P_KT = bank("P_KT")
        P_AT = bank("P_AT")
        P_PJ = bank("P_PJ")

        P_W = [P_MAX[0], P_MAX[1], P_EXP[0], P_EXP[1]]
        P_H = [P_MAX[0], P_MAX[1], P_KT]
        P_O = [P_EXP[0], P_EXP[1], P_AT, P_PJ]
        P_YT = P_QT

        def as_bf16(t):
            return t[:, :].bitcast(bf16)

        x_in = [sem(f"x_in{c}") for c in range(5)]
        ctx_in = [sem(f"ctx_in{c}") for c in range(2)]
        bc_in, wc_in, w1_in, w2_in, sa_in, bias_in = (sem(n) for n in ("bc_in", "wc_in", "w1_in", "w2_in", "sa_in", "bias_in"))
        zeroed, consts_ready = sem("zeroed"), sem("consts_ready")
        ones_done = sem("ones_done")
        st1_done, mv1_done, ve1_done, rs1_done, q_done = (sem(n) for n in ("st1_done", "mv1_done", "ve1_done", "rs1_done", "q_done"))
        part1_done, rest_done, part2_done, part3_done = (sem(n) for n in ("part1_done", "rest_done", "part2_done", "part3_done"))
        nm1_done = sem("nm1_done")
        xb_done, v1_done = sem("xb_done"), sem("v1_done")
        qt_done, qs0_done, qs1_done = sem("qt_done"), sem("qs0_done"), sem("qs1_done")
        kt_done, ks_done = sem("kt_done"), sem("ks_done")
        smax_done, max_done, nmp1_done, nmp2_done = sem("smax_done"), sem("max_done"), sem("nmp1_done"), sem("nmp2_done")
        nmt_done, nmts_done = sem("nmt_done"), sem("nmts_done")
        nm_row = [sem("nm_row0"), sem("nm_row1")]
        sexp_done, exp_done, at_done, ats_done = sem("sexp_done"), sem("exp_done"), sem("at_done"), sem("ats_done")
        back_done, rsum_done, on_done, ont_done, onts_done = (sem(n) for n in ("back_done", "rsum_done", "on_done", "ont_done", "onts_done"))
        proj_done, x1_done, st2_done, mv2_done = sem("proj_done"), sem("x1_done"), sem("st2_done"), sem("mv2_done")
        ve2_done, rs2_done, rq2_done = sem("ve2_done"), sem("rs2_done"), sem("rq2_done")
        ya_done, yb_done, y_done = sem("ya_done"), sem("yb_done"), sem("y_done")
        wct_done, wcts_done = sem("wct_done"), sem("wcts_done")
        amax_done, amaxall_done, scales = sem("amax_done"), sem("amaxall_done"), sem("scales")
        wm_done, wq_done, wt_done, wts_done = sem("wm_done"), sem("wq_done"), sem("wt_done"), sem("wts_done")
        bias_steps = sem("bias_steps")
        x1b_done, warm_done = sem("x1b_done"), sem("warm_done")
        yt_done, yts_done, h_done, relu_done, hm_done, hq_done = (sem(n) for n in ("yt_done", "yts_done", "h_done", "relu_done", "hm_done", "hq_done"))
        o_done, res_done = [sem(f"o_done{s}") for s in range(BG)], sem("res_done")
        out_sent = [sem("out_sent0"), sem("out_sent1")]

        AHEAD = {NB + 1: ((), (), (0, 1)), NB + 2: ((2,), (3, 4), (5, 6)), NB + 3: ((7, 8), (9,), (10, 11))}
        FIRST = AHEAD[NB + LAST - 1][2][-1] + 1
        TURN = [2] * (NG - 1) + [NF]
        BEHIND = 3
        SKEW = 1
        parts_due = {}
        EARLY = [(k, s) for k in range(4) for s in (0, 1)]
        done = [4, 4, 0, 0]
        ended = []
        for i in range(FIRST, NT + 1):
            base = (i + 1 - FIRST) * (NT - BEHIND) // (NT - FIRST) if i < NT else NT
            parts_due[i] = []
            resting, ended = ended, []
            for k in range(NT):
                for s in range(BG):
                    if done[s] == k and s not in ended + resting and k < (base - min(SKEW * s, NT - BEHIND - base) if i < NT else NT):
                        parts_due[i].append((k, s))
                        done[s] += 1
                        if done[s] % NF == 0 and i < NT:
                            ended.append(s)
            begin = [s for k, s in parts_due[i] if k % NF == 0]
            parts_due[i].sort(key=lambda ks: (ks[1] in begin, ks[0]))

        NORMS = {1: (4,), 2: (5,), 3: (6,), 4: (7,), 5: (8, 9), 6: (10, 11), 7: (12, 13, 14, 15)}
        CH = [(0, 1), (1, 4), (4, 8), (8, 12), (12, 16)]
        CC = [(0, 4), (4, 16)]
        AMX, RMX, SW, SS, RSS, CH_, RSA1, RSA2 = 0, 2, 4, 6, 8, 10, 11, 12

        QH, KH = slice(0, H), slice(H, NH)
        QSLOTS = {1: (QH, slice(0, 3)), 2: (QH, slice(3, 5)), 3: (QH, slice(5, 6))}
        KSLOTS = {1: (KH, slice(1, 6, 2)), 2: (KH, slice(0, 5, 4)), 3: (KH, slice(2, 3))}

        def static(b):
            return isinstance(b, int)

        def there(b, first=0, last=NB - 1):
            return not static(b) or first <= b <= last

        def wait(eng, s, value):
            if not static(value) or value > 0:
                eng.wait_ge(s, value)

        def pipeline(eng, step, head=None, first=RING, last=LAST):
            head = head or (lambda it, u: None)
            for it in range(first):
                head(it, it % RING)
                step(it, it % RING)
            head(first, 0)
            with eng.Fori(first // RING, NB // RING) as k:
                for u in range(RING):
                    step(k * RING + u, u)
                    head(k * RING + u + 1, (u + 1) % RING)
            for it in range(NB, NB + last):
                step(it, it % RING)
                head(it + 1, (it + 1) % RING)

        def nm_rows(it, u, lag):
            return (it - u) * 8 + 16 * ((u - lag) // 2 + 1)

        block = es.enter_context(nc.Block())

        @block.sync
        def _(sp):
            def load_x(c):
                a, b = CH[c]
                sp.dma_start(X[:, a:b, :], x[a:b].rearrange("b s d -> s b d")).then_inc(x_in[c], 16)

            def load_ctx(c):
                a, b = CC[c]
                sp.dma_start(QK[:, a:b, D:W], ctx_512[a:b].rearrange("b s d -> s b d")).then_inc(ctx_in[c], 16)
            load_x(0)
            load_ctx(0)
            load_x(1)
            load_x(2)
            sp.dma_start(W1R[:, :, :], W1.rearrange("(j p) k -> p j k", p=128)).then_inc(w1_in, 16)
            sp.dma_start(BC[:, :], bc.rearrange("(a n) -> a n", a=1).to_broadcast([S, D])).then_inc(bc_in, 16)
            sp.dma_start(SA[:, 0:1], s_act1.rearrange("(a n) -> a n", a=1).to_broadcast([128, 1])).then_inc(sa_in, 16)
            sp.dma_start(SA[:, 1:2], s_act2.rearrange("(a n) -> a n", a=1).to_broadcast([128, 1])).then_inc(sa_in, 16)
            load_x(3)
            sp.dma_start(W2R[:, :, :], W2.rearrange("(j p) k -> p j k", p=128)).then_inc(w2_in, 16)
            load_ctx(1)
            load_x(4)
            sp.dma_start(WCR[:, :, :], Wc.rearrange("(j p) k -> p j k", p=128)).then_inc(wc_in, 16)
            sp.dma_start(B12[:, NF:], b2.rearrange("(a n) -> a n", a=1).to_broadcast([S, D])).then_inc(bias_in, 16)
            with nc.allow_non_contiguous_dma(reason="1024 biases, one to a partition and tile"):
                sp.dma_start(B12[:, 0:NF], b1.rearrange("(j p) -> p j", p=128)).then_inc(bias_in, 16)

            def step(it, u):
                b, r = it - 2, (u - 2) % RING
                if there(b):
                    sp.wait_ge(nmts_done, b + 1)
                    sp.dma_start(QS[KR:KM, r, :, :], NMT[:, r % 2, :]).then_inc(nm_row[r % 2], 16)
            pipeline(sp, step)

            for n in range(NG):
                for a, b in ((0, BG),) if n < NG - 1 else ((0, BG // 2), (BG // 2, BG)):
                    sp.wait_ge(res_done, BG * n + b)
                    sp.dma_start(out[n * BG + a:n * BG + b].rearrange("b s d -> s b d"),
                                 OUT[:, n % 2, a:b, :]).then_inc(out_sent[n % 2], 16)
            sp.wait_ge(out_sent[0], 16 * (NG // 2))
            sp.wait_ge(out_sent[1], 16 * (NG // 2 + 1))

        @block.gpsimd
        def _(pool):
            pool.memset(HALF[:, :], -0.5).then_inc(zeroed, 1)
            pool.memset(EPST[:, :], EPS).then_inc(zeroed, 1)
            pool.memset(IDF[:, :], 0.0).then_inc(zeroed, 1)
            pool.memset(IDB[:, :], 0.0).then_inc(zeroed, 1)
            pool.memset(MAG[:, :], MAGIC).then_inc(consts_ready, 1)
            pool.wait_ge(zeroed, 4)
            for t in (IDF, IDB):
                pool.affine_select(out=t[:, :], in_=t[:, :], compare_op=ALU.not_equal, fill=1.0, base=0,
                                   pattern=[[-1, 128]], channel_multiplier=1).then_inc(consts_ready, 1)

            def rstd1(c):
                a, b = CH[c]
                pool.wait_ge(mv1_done, b)
                pool.tensor_scalar(VE1[:, a:b], MV1[:, a:b, 1], EPS, float(HD), ALU.add, ALU.mult).then_inc(ve1_done, 1)
                pool.wait_ge(ve1_done, c + 1)
                pool.tensor_tensor(RS1[:, a:b], VE1[:, a:b], HALF[:, a:b], ALU.pow).then_inc(rs1_done, 1)
                if c >= 2:
                    pool.tensor_scalar(NM1[:, a:b], MV1[:, a:b, 0], -1.0, 0.0, ALU.mult, ALU.add).then_inc(nm1_done, 1)
                    pool.wait_ge(nm1_done, c - 1)
                    pool.wait_ge(rs1_done, c + 1)

            def norm1(batches):
                for i in batches:
                    pool.wait_ge(q_done, i)
                    pool.tensor_scalar(QK[:, i, 0:D], X[:, i, :], NM1[:, i:i + 1], RS1[:, i:i + 1],
                                       ALU.add, ALU.mult).then_inc(q_done, 1)
                if batches[-1] == NB - 1:
                    pool.wait_ge(q_done, NB)
                    pool.memset(QK[:, NB, :], 0.0).then_inc(q_done, 1)

            rstd1(0)
            pool.memset(V1[:, :, :, HD:32], 0.0).then_inc(zeroed, 1)
            pool.wait_ge(zeroed, 5)
            pool.memset(V1[:, :, :, HD:HD + 1], 1.0).then_inc(v1_done, 1)

            def rest(b, r):
                pool.wait_ge(part1_done, 2 * (b + 1))
                wait(pool, part3_done, 2 * (b - 1))
                pool.tensor_tensor(REST[:, r % 2, :].rearrange("p (h d) -> p h d", d=HD),
                                   QK[:, b, :].rearrange("p (h d) -> p h d", d=HD),
                                   PARTS[:, r % 2, :, 1, :], ALU.subtract).then_inc(rest_done, 1)

            def part3(b, r):
                pool.wait_ge(part2_done, 2 * (b + 1))
                rest_ = REST[:, r % 2, :].rearrange("p (h d) -> p h d", d=HD)
                for hs, slot in QSLOTS[3], KSLOTS[3]:
                    pool.tensor_tensor(PARTS[:, r % 2, hs, slot, :], rest_[:, hs, :].unsqueeze(2), PARTS[:, r % 2, hs, 4:5, :],
                                       ALU.subtract).then_inc(part3_done, 1)

            def biases(w):
                B, T = (B12[:, 0:NF], TB[:, 0:NF]) if w == 0 else (B12[:, NF:], TB[:, NF:])
                after = (SC[:, CH_:CH_ + 1], SC[:, SS + 1:SS + 2])[w]
                count = [7 * w]

                def then(ins):
                    count[0] += 1
                    ins.then_inc(bias_steps, 1)
                    pool.wait_ge(bias_steps, count[0])
                pool.wait_ge(bias_in, 32)
                pool.wait_ge(scales, 9)
                then(pool.tensor_tensor(B, B, SC[:, RSS + w:RSS + w + 1].to_broadcast(list(B.shape)), ALU.mult))
                then(pool.tensor_scalar(T, B, IMAX, -IMAX, ALU.min, ALU.max))
                then(pool.tensor_tensor(B, B, T, ALU.subtract))
                then(pool.tensor_scalar(T, T, MAGIC, MAGIC, ALU.add, ALU.subtract))
                then(pool.tensor_tensor(B, B, T, ALU.add))
                then(pool.tensor_scalar(B, B, 2.0 ** 31, -2.0 ** 31, ALU.min, ALU.max))
                then(pool.tensor_tensor(B, B, after.to_broadcast(list(B.shape)), ALU.mult))

            def plus_b2(n):
                for b in range(n * BG, (n + 1) * BG):
                    pool.wait_ge(y_done, b + 1)
                    pool.tensor_tensor(X1[:, b, :], X1[:, b, :], B12[:, NF:], ALU.add).then_inc(x1b_done, 1)

            rest(0, 0)
            rstd1(1)
            part3(0, 0)
            rstd1(2)
            pool.wait_ge(bc_in, 16)

            def step(it, u):
                if there(it + 1, 0, NB):
                    rest(it + 1, (u + 1) % RING)
                if there(it):
                    pool.wait_ge(q_done, it + 1)
                    pool.tensor_tensor(X[:, it, :], X[:, it, :], BC[:, :], ALU.add).then_inc(xb_done, 1)
                if there(it - 5):
                    b, r = it - 5, (u - 5) % RING
                    pool.wait_ge(mv2_done, b + 1)
                    pool.tensor_tensor(VE2[:, r:r + 1], MV2[:, r, 1:2], EPST[:, :], ALU.add).then_inc(ve2_done, 1)
                    pool.wait_ge(ve2_done, b + 1)
                    pool.tensor_tensor(RS2[:, r:r + 1], VE2[:, r:r + 1], HALF[:, 0:1], ALU.pow).then_inc(rs2_done, 1)
                    if static(b) and b == 0:
                        pool.wait_ge(scales, 1)
                    pool.wait_ge(rs2_done, b + 1)
                    pool.tensor_tensor(RQ2[:, r:r + 1], RS2[:, r:r + 1], SC[:, RSA1:RSA1 + 1], ALU.mult).then_inc(rq2_done, 1)
                if there(it - 2):
                    b, r = it - 2, (u - 2) % RING
                    wait(pool, at_done, b - 1)
                    pool.wait_ge(ctx_in[0 if static(b) and b < CC[0][1] else 1], 16)
                    pool.tensor_copy(V1[:, r % 2, :, 0:HD],
                                     QK[:, b, D:W].rearrange("p (g d) -> p g d", g=G)).then_inc(v1_done, 1)
                if there(it + 1, 0, NB):
                    part3(it + 1, (u + 1) % RING)
                if static(it) and it in (1, 2):
                    w = it - 1
                    pool.wait_ge(amax_done, w + 1)
                    pool.partition_all_reduce(AMAX[:, w:w + 1], SC[:, AMX + w:AMX + w + 1], 128, RMAX).then_inc(amaxall_done, 2)
                if static(it) and it in NORMS:
                    norm1(NORMS[it])
                if static(it) and it in (4, 6):
                    rstd1(it // 2 + 1)
                if static(it) and it in (NB, NB + 1):
                    biases(it - NB)
                if static(it) and it > NB + 1:
                    plus_b2(it - NB - 2)
            pipeline(pool, step, first=2 * RING, last=LAST + 1)
            plus_b2(3)

        @block.vector
        def _(dve):
            vec = nc.vector
            vec.memset(KS[KR:KM, :, :, :], 1.0).then_inc(ones_done, 1)

            def stats1(a, b):
                for c, (first, _) in enumerate(CH):
                    if first in range(a, b):
                        dve.wait_ge(x_in[c], 16)
                for i in range(a, b):
                    vec.bn_stats(ST1[:, i, :], X[:, i, :]).then_inc(st1_done, 1)
                for i in range(a, b):
                    dve.wait_ge(st1_done, i + 1)
                    vec.bn_aggr(MV1[:, i, :], ST1[:, i, :]).then_inc(mv1_done, 1)

            def norm1(c):
                a, b = CH[c]
                dve.wait_ge(rs1_done, c + 1)
                for i in range(a, b):
                    vec.tensor_scalar(QK[:, i, 0:D], X[:, i, :], MV1[:, i, 0:1], RS1[:, i:i + 1],
                                      ALU.subtract, ALU.mult).then_inc(q_done, 1)

            def small(ins, n):
                ins.then_inc(scales, 1)
                dve.wait_ge(scales, n)

            def abs_max(w):
                dve.wait_ge((w1_in, w2_in)[w], 16)
                vec.tensor_reduce(SC[:, AMX + w:AMX + w + 1], (W1R, W2R)[w][:, :, :], AX.XY, ALU.max,
                                  apply_absolute_value=True).then_inc(amax_done, 1)

            stats1(*CH[0])
            norm1(0)
            stats1(*CH[1])
            norm1(1)
            stats1(*CH[2])
            dve.wait_ge(sa_in, 32)
            small(vec.reciprocal(SC[:, RSA1:RSA1 + 2], SA[:, 0:2]), 1)

            def row_max(b, r, g):
                i = b * HG + g
                dve.wait_ge(smax_done, i + 1)
                if g == 0:
                    wait(dve, nmp2_done, b - 1)
                vec.tensor_reduce(NMAX[:, r % 2, g * HG:(g + 1) * HG],
                                  P_MAX[g % 2][:, :].rearrange("p (h t) -> p h t", t=S),
                                  AX.X, ALU.max, negate=True).then_inc(max_done, 1)

            def head(it, u):
                late = there(it - 5)
                b5, r5 = it - 5, (u - 5) % RING
                if late:
                    dve.wait_ge(proj_done, b5 + 1)
                    dve.wait_ge(xb_done, b5 + 1)
                    vec.tensor_tensor(X1[:, b5, :], P_PJ[:, D:2 * D], X[:, b5, :], ALU.add).then_inc(x1_done, 1)
                    dve.wait_ge(x1_done, b5 + 1)
                if there(it - 4):
                    b = it - 4
                    dve.wait_ge(back_done, b + 1)
                    back = P_AT[:, :].rearrange("p (h g e) -> p h g e", h=HG, g=G)
                    vec.reciprocal(RSUM[:, :].rearrange("p (h g) -> p h g", h=HG), back[:, :, :, HD]).then_inc(rsum_done, 1)
                    if late:
                        vec.bn_stats(ST2[:, r5, :], X1[:, b5, :]).then_inc(st2_done, 1)
                    dve.wait_ge(rsum_done, b + 1)
                    wait(dve, ont_done, b)
                    vec.tensor_tensor(ON[:, :, :, :].rearrange("p g h d -> p h g d"), back[:, :, :, 0:HD],
                                      RSUM[:, :].rearrange("p (h g) -> p h g", h=HG).unsqueeze(3).to_broadcast([S, HG, G, HD]),
                                      ALU.mult).then_inc(on_done, 1)
                if late and not there(it - 4):
                    vec.bn_stats(ST2[:, r5, :], X1[:, b5, :]).then_inc(st2_done, 1)
                if late:
                    dve.wait_ge(st2_done, b5 + 1)
                if there(it - 1):
                    row_max(it - 1, (u - 1) % RING, 0)
                if late:
                    vec.bn_aggr(MV2[:, r5, :], ST2[:, r5, :]).then_inc(mv2_done, 1)
                    ahead(it - 1, 2)
                if there(it - 1):
                    row_max(it - 1, (u - 1) % RING, 1)

            def norm2(b5, r5):
                dve.wait_ge(rq2_done, b5 + 1)
                wait(dve, yb_done, b5)
                vec.tensor_scalar(YA[:, r5 % 2, :], X1[:, b5, :], MV2[:, r5, 0:1], RQ2[:, r5:r5 + 1],
                                  ALU.subtract, ALU.mult).then_inc(ya_done, 1)

            def clip2(b5, r5):
                dve.wait_ge(ya_done, b5 + 1)
                wait(dve, y_done, b5)
                vec.tensor_scalar(YB[:, r5 % 2, :], YA[:, r5 % 2, :], QMAX, QMIN, ALU.min, ALU.max).then_inc(yb_done, 1)

            def round2(b5, r5):
                dve.wait_ge(yb_done, b5 + 1)
                vec.tensor_scalar(Y[:, b5, :], YB[:, r5 % 2, :], MAGIC, MAGIC, ALU.add, ALU.subtract).then_inc(y_done, 1)

            def step(it, u):
                r = u % RING
                b1_, r1 = it - 1, (u - 1) % RING
                if static(it):
                    extra(it)
                if there(b1_):
                    row_max(b1_, r1, 2)
                    row_max(b1_, r1, 3)
                    dve.wait_ge(max_done, HG * (b1_ + 1))
                    wait(dve, nmt_done, b1_ - 1)
                    vec.tensor_copy(NMP[:, r1 % 2, 0:H], NMAX[:, r1 % 2, :]).then_inc(nmp1_done, 1)
                b5, r5 = it - 5, (u - 5) % RING
                if there(b5) and not (static(it) and it > NB):
                    norm2(b5, r5)
                if there(it):
                    dve.wait_ge(qt_done, 2 * it + 2)
                    wait(dve, sexp_done, G * (it - RING + 1))
                    vec.tensor_copy(QS[0:KR, r, H // 2:H, :],
                                    as_bf16(P_QT)[0:KR, :].rearrange("p (h s) -> p h s", s=S)).then_inc(qs1_done, 1)
                if there(b5) and not (static(it) and it > NB):
                    clip2(b5, r5)
                if there(b1_):
                    dve.wait_ge(nmp1_done, b1_ + 1)
                    vec.tensor_tensor(NMP[:, r1 % 2, H:2 * H], NMAX[:, r1 % 2, :], NMP[:, r1 % 2, 0:H],
                                      ALU.subtract).then_inc(nmp2_done, 1)
                if there(b5) and not (static(it) and it > NB):
                    round2(b5, r5)
                ahead(it, 0)
                ahead(it, 1)
                if static(it) and it > NB + 1:
                    norm2(it - 6, (it - 6) % RING)
                    clip2(it - 6, (it - 6) % RING)
                    round2(it - 6, (it - 6) % RING)
                if static(it) and it == NB + 2:
                    w_out(1)

            def extra(it):
                if it == 1:
                    abs_max(0)
                if it == 2:
                    inverse_scale(0)
                    abs_max(1)
                if it == 3:
                    dve.wait_ge(wct_done, 1)
                    vec.tensor_copy(WCT[:, :, :], P_PJ[:, :].rearrange("p (j n) -> p j n", j=DH)).then_inc(wcts_done, 1)
                    inverse_scale(1)
                if 3 <= it <= 6:
                    stats1(2 * it + 2, 2 * it + 4)
                if it == 4:
                    scales_of_products()
                if it == 3:
                    w_int(0)
                if it == NB + 1:
                    w_out(0)
                    w_int(1)

            def ahead(it, place):
                if static(it) and it in AHEAD:
                    for i in AHEAD[it][place]:
                        quantise(i)

            def w_int(w):
                dve.wait_ge(wm_done, w + 1)
                src, dst = ((W1R, W1Q), (W2R, W2Q))[w]
                vec.tensor_scalar(dst[:, :, :], src[:, :, :], MAGIC, 1.0, ALU.subtract, ALU.mult).then_inc(wq_done, 1)

            def w_out(w):
                for j in range(2):
                    i = 2 * w + j
                    dve.wait_ge(wt_done, i + 1)
                    src = as_bf16(P_W[i])[:, :]
                    if w == 0:
                        vec.tensor_copy(W1T[:, j, :], src).then_inc(wts_done, 1)
                    else:
                        vec.tensor_copy(W2T[:, j * NF // 2:(j + 1) * NF // 2, :],
                                        src.rearrange("p (f k) -> p f k", k=D)).then_inc(wts_done, 1)

            def inverse_scale(w):
                dve.wait_ge(amaxall_done, 2 * (w + 1))
                c = RMX + w
                small(vec.reciprocal(SC[:, c:c + 1], AMAX[:, w:w + 1]), 2 * w + 2)
                small(vec.tensor_scalar(SC[:, c:c + 1], SC[:, c:c + 1], QMAX, 1.0, ALU.mult, ALU.mult), 2 * w + 3)

            def scales_of_products():
                small(vec.tensor_scalar(SC[:, SW:SW + 2], AMAX[:, :], 1.0 / QMAX, 1.0, ALU.mult, ALU.mult), 6)
                small(vec.tensor_tensor(SC[:, SS:SS + 2], SA[:, :], SC[:, SW:SW + 2], ALU.mult), 7)
                vec.tensor_tensor(SC[:, CH_:CH_ + 1], SC[:, SS:SS + 1], SC[:, RSA2:RSA2 + 1], ALU.mult).then_inc(scales, 1)
                small(vec.reciprocal(SC[:, RSS:RSS + 2], SC[:, SS:SS + 2]), 9)

            def quantise(i):
                if i < NT:
                    dve.wait_ge(relu_done, i + 1)
                    wait(dve, hq_done, i - 3)
                    vec.tensor_scalar(HM[:, i % 4, :], HF[:, i % 4, :], UMAX, MAGIC, ALU.min, ALU.add).then_inc(hm_done, 1)
                if i > 0:
                    k = i - 1
                    dve.wait_ge(hm_done, k + 1)
                    wait(dve, o_done[BG - 1], k - 2 * NF + 1)
                    vec.tensor_scalar(HQ[:, k // NF % 2, k % NF, :], HM[:, k % 4, :], MAGIC, 1.0,
                                      ALU.subtract, ALU.mult).then_inc(hq_done, 1)

            def result(n, s):
                b = n * BG + s
                dve.wait_ge(o_done[s], NF * (n + 1))
                dve.wait_ge(x1b_done, b + 1)
                if s == 0 and n >= 2:
                    dve.wait_ge(out_sent[n % 2], 16 * (n // 2))
                vec.scalar_tensor_tensor(out=OUT[:, n % 2, s, :], in0=P_O[s][:, 0:D], scalar=SC[:, SS + 1:SS + 2],
                                         in1=X1[:, b, :], op0=ALU.mult, op1=ALU.add).then_inc(res_done, 1)

            pipeline(dve, step, head, first=2 * RING, last=LAST + 1)
            for i in range(FIRST, NT + 1):
                if i >= NT - 1:
                    quantise(i)
                for k, s in parts_due[i - 1] if i > FIRST else ():
                    if k % NF == NF - 1:
                        result(k // NF, s)
                if i < NT - 1:
                    quantise(i)
                if i == FIRST + 2:
                    norm2(NB - 1, (NB - 1) % RING)
                    clip2(NB - 1, (NB - 1) % RING)
                    round2(NB - 1, (NB - 1) % RING)
            for k, s in parts_due[NT]:
                if k % NF == NF - 1:
                    result(k // NF, s)


        @block.scalar
        def _(act):
            sc = nc.scalar

            def part1(b, r):
                act.wait_ge(q_done, b + 1)
                act.wait_ge(ctx_in[0 if static(b) and b < CC[0][1] else 1], 16)
                wait(act, qt_done, 2 * (b - 1))
                wait(act, kt_done, b - 1)
                spread(QK[:, b, :], r, 1, part1_done)

            def spread(value, r, part, done):
                value = value.rearrange("p (h d) -> p h d", d=HD)
                for hs, slots in QSLOTS[part], KSLOTS[part]:
                    to = PARTS[:, r % 2, hs, slots, :]
                    sc.copy(to, value[:, hs, :].unsqueeze(2).to_broadcast(list(to.shape))).then_inc(done, 1)

            def part2(b, r):
                act.wait_ge(rest_done, b + 1)
                spread(REST[:, r % 2, :], r, 2, part2_done)

            def exps(b, r, gs):
                for g in gs:
                    act.wait_ge(sexp_done, G * b + g + 1)
                    if g == 0:
                        wait(act, at_done, b - 1)
                    sc.activation(PR[:, r % 2, g, :], P_EXP[g % 2][:, :], ACT.Exp).then_inc(exp_done, 1)

            act.wait_ge(consts_ready, 1)
            sc.activation(WARM[:, :], MAG[:, :], ACT.Exp, scale=0.0).then_inc(warm_done, 1)
            part1(0, 0)
            part2(0, 0)

            def step(it, u):
                if there(it - 4):
                    b = it - 4
                    act.wait_ge(at_done, b + 1)
                    wait(act, back_done, b)
                    sc.copy(OT[:, :], P_AT[:, :]).then_inc(ats_done, 1)
                ahead(it - 1, 2)
                if there(it - 3):
                    exps(it - 3, (u - 3) % RING, (0, 1))
                if there(it + 1, 0, NB):
                    part1(it + 1, (u + 1) % RING)
                if static(it) and it == NB + 1:
                    max_turned(it, u)
                ahead(it, 0)
                if there(it - 3):
                    exps(it - 3, (u - 3) % RING, (2, 3))
                if there(it - 2) and not (static(it) and it == NB + 1):
                    max_turned(it, u)
                if there(it):
                    r = u % RING
                    act.wait_ge(qt_done, 2 * it + 1)
                    wait(act, sexp_done, G * (it - RING + 1))
                    sc.copy(QS[0:KR, r, 0:H // 2, :],
                            as_bf16(P_QT)[0:KR, :].rearrange("p (h s) -> p h s", s=S)).then_inc(qs0_done, 1)
                if there(it - 4):
                    b = it - 4
                    act.wait_ge(ont_done, b + 1)
                    wait(act, proj_done, b)
                    sc.copy(ONT[:, :, :], P_PJ[:, 0:D].rearrange("p (j s) -> p j s", j=DH)).then_inc(onts_done, 1)
                if there(it):
                    act.wait_ge(kt_done, it + 1)
                    wait(act, sexp_done, G * (it - RING + 1))
                    sc.copy(KS[0:KR, r, :, :], as_bf16(P_KT)[0:KR, 0:G * S].rearrange("p (g t) -> p g t", t=S)).then_inc(ks_done, 1)
                if static(it) and it == NB + 1:
                    turned(0)
                ahead(it, 1)
                if there(it + 1, 0, NB):
                    part2(it + 1, (u + 1) % RING)
                if static(it) and it in (W1_STEP, NB):
                    w = int(it == NB)
                    act.wait_ge(scales, 3 + 2 * w)
                    t = (W1R, W2R)[w]
                    sc.activation(t[:, :, :], t[:, :, :], ACT.Identity, bias=MAG[:, 0:1],
                                  scale=SC[:, RMX + w:RMX + w + 1]).then_inc(wm_done, 1)

            def max_turned(it, u):
                b, r = it - 2, (u - 2) % RING
                act.wait_ge(nmt_done, b + 1)
                wait(act, nm_row[r % 2], nm_rows(it, u, 4))
                sc.copy(NMT[:, r % 2, :], as_bf16(P_KT)[0:2 * H, 0:S]).then_inc(nmts_done, 1)

            def ahead(it, place):
                if static(it) and it in AHEAD:
                    for i in AHEAD[it][place]:
                        relu(i)

            def turned(n):
                act.wait_ge(yt_done, n + 1)
                wait(act, h_done, NF * (n - 1))
                sc.copy(YT[:, n % 2, :, :], as_bf16(P_YT)[:, :].rearrange("p (j s) -> p j s", j=DH)).then_inc(yts_done, 1)

            def relu(i):
                n, f = i // NF, i % NF
                act.wait_ge(h_done, i + 1)
                if i == 0:
                    act.wait_ge(bias_steps, 7)
                wait(act, hm_done, i - 3)
                sc.activation(HF[:, i % 4, :], P_H[i % 3][:, :], ACT.Relu, bias=B12[:, f:f + 1],
                              scale=SC[:, CH_:CH_ + 1]).then_inc(relu_done, 1)
                if f == TURN[n] + 2:
                    turned(n + 1)

            pipeline(act, step, first=2 * RING)
            ahead(NB + LAST - 1, 2)
            for i in range(FIRST, NT):
                relu(i)

        @block.tensor
        def _(pe):
            mm, tr = nc.tensor.matmul, nc.tensor.transpose

            def q_turn(b, r, half):
                for j in range(H // 2):
                    last = tr(as_bf16(P_QT)[0:KR, j * S:(j + 1) * S],
                              PARTS[:, r % 2, half * (H // 2) + j, :, :].rearrange("p c d -> p (c d)"), IDB[:, :])
                last.then_inc(qt_done, 1)

            def k_turn(b, r):
                for g in range(G):
                    last = tr(as_bf16(P_KT)[0:KR, g * S:(g + 1) * S],
                              PARTS[:, r % 2, H + g, :, :].rearrange("p c d -> p (c d)"), IDB[:, :])
                last.then_inc(kt_done, 1)

            def scores_max(b, r, g):
                i = HG * b + g
                wait(pe, max_done, i - 1)
                for hh in range(HG):
                    last = mm(P_MAX[g % 2][:, hh * S:(hh + 1) * S], QS[0:KR, r, g * HG + hh, :], KS[0:KR, r, g, :],
                              start=True, stop=True)
                last.then_inc(smax_done, 1)

            def scores_exp(b, r, g):
                i = HG * b + g
                wait(pe, exp_done, i - 1)
                mm(P_EXP[g % 2][:, :], KS[:, r, g, :], QS[:, r, g * HG:(g + 1) * HG, :],
                   start=True, stop=True).then_inc(sexp_done, 1)

            pe.wait_ge(consts_ready, 3)

            def head(it, u):
                b3_, r3, b5_ = it - 3, (u - 3) % RING, it - 5
                if static(it) and it > NB + 1:
                    project(b5_)
                if there(b3_):
                    if static(b3_) and b3_ == 0:
                        pe.wait_ge(ones_done, 1)
                    pe.wait_ge(nm_row[r3 % 2], nm_rows(it, u, 3))
                    for g in (0, 1):
                        scores_exp(b3_, r3, g)
                if there(b5_) and not (static(it) and (it == LAST or it > NB + 1)):
                    project(b5_)

            def max_turn(b, r):
                tr(as_bf16(P_KT)[0:2 * H, 0:S], NMP[:, r % 2, :], IDB[:, :]).then_inc(nmt_done, 1)

            def project(b5_):
                pe.wait_ge(onts_done, b5_ + 1)
                for j in range(DH):
                    last = mm(P_PJ[:, D:2 * D], ONT[:, j, :], WCT[:, j, :], start=(j == 0), stop=(j == DH - 1))
                last.then_inc(proj_done, 1)

            def step(it, u):
                b1_, b2_, b3_, b4_ = (it - l for l in (1, 2, 3, 4))
                r1, r2, r3, r4 = ((u - l) % RING for l in (1, 2, 3, 4))
                if there(b4_):
                    pe.wait_ge(ats_done, b4_ + 1)
                    for hh in range(HG):
                        last = tr(P_AT[:, hh * S:(hh + 1) * S], OT[:, hh * S:(hh + 1) * S], IDF[:, :])
                    last.then_inc(back_done, 1)
                ahead(it, 0)
                if there(b3_):
                    for g in (2, 3):
                        scores_exp(b3_, r3, g)
                if static(it) and it == NB + 1:
                    weights(0)
                if there(b1_):
                    pe.wait_ge(ks_done, b1_ + 1)
                    pe.wait_ge(qs0_done, b1_ + 1)
                    for g in (0, 1):
                        scores_max(b1_, r1, g)
                if there(b2_) and not (static(it) and it == NB + 1):
                    pe.wait_ge(nmp2_done, b2_ + 1)
                    wait(pe, ks_done, it)
                    max_turn(b2_, r2)
                if there(it):
                    pe.wait_ge(part3_done, 2 * (it + 1))
                    wait(pe, qs1_done, it)
                    q_turn(it, u, 0)
                if there(b4_):
                    pe.wait_ge(on_done, b4_ + 1)
                    wait(pe, x1_done, b4_)
                    if static(b4_) and b4_ == 0:
                        pe.wait_ge(wcts_done, 1)
                    on = ON[:, :, :, :].rearrange("p g h d -> p (g h d)")
                    for j in range(DH):
                        last = tr(P_PJ[:, j * S:(j + 1) * S], on[:, j * 128:(j + 1) * 128], IDF[:, :])
                    last.then_inc(ont_done, 1)
                if static(it) and it == NB + 1:
                    turn(0)
                if static(it) and it == NB + 3:
                    for k, s in EARLY:
                        output(k, s)
                ahead(it, 1)
                if there(it):
                    wait(pe, nmts_done, it - 1)
                    k_turn(it, u)
                if there(b1_):
                    pe.wait_ge(qs1_done, b1_ + 1)
                    for g in (2, 3):
                        scores_max(b1_, r1, g)
                if there(b3_):
                    pe.wait_ge(exp_done, G * (b3_ + 1))
                    pe.wait_ge(v1_done, b3_ + 2)
                    wait(pe, on_done, b3_)
                    for g in range(G):
                        last = mm(P_AT[32 * g:32 * (g + 1), :], V1[:, r3 % 2, g, :], PR[:, r3 % 2, g, :],
                                  start=True, stop=True, tile_position=(0, 32 * g))
                    last.then_inc(at_done, 1)
                if there(it):
                    pe.wait_ge(qs0_done, it + 1)
                    q_turn(it, u, 1)
                if static(it) and it == 1:
                    pe.wait_ge(wc_in, 16)
                    for j in range(DH):
                        for m in range(DH):
                            last = tr(P_PJ[:, j * D + m * 128:j * D + (m + 1) * 128],
                                      WCR[:, m, j * 128:(j + 1) * 128], IDF[:, :])
                    last.then_inc(wct_done, 1)
                if static(it) and it == NB:
                    pe.wait_ge(nmts_done, NB - 1)
                    pe.wait_ge(nmp2_done, NB)
                    max_turn(NB - 1, (NB - 1) % RING)
                if static(it) and it == NB + 2:
                    weights(1)
                ahead(it, 2)

            def ahead(it, place):
                if static(it) and it in AHEAD:
                    for i in AHEAD[it][place]:
                        hidden(i)

            def weights(w):
                pe.wait_ge(wq_done, w + 1)
                for j in range(2):
                    if w == 0:
                        pe.wait_ge(max_done, HG * NB)
                    else:
                        pe.wait_ge(exp_done, G * NB)
                    for m in range(NF):
                        if w == 0:
                            src = W1Q[:, m, j * 128:(j + 1) * 128]
                        else:
                            f, dh = j * NF // 2 + m // DH, m % DH
                            src = W2Q[:, dh, f * 128:(f + 1) * 128]
                        last = tr(as_bf16(P_W[2 * w + j])[:, m * 128:(m + 1) * 128], src, IDB[:, :])
                    last.then_inc(wt_done, 1)

            def turn(n):
                pe.wait_ge(y_done, BG * (n + 1))
                wait(pe, yts_done, n)
                if n == 0:
                    pe.wait_ge(qs1_done, NB)
                for j in range(DH):
                    for s in range(BG):
                        last = tr(as_bf16(P_YT)[:, (j * BG + s) * S:(j * BG + s + 1) * S],
                                  Y[:, n * BG + s, j * 128:(j + 1) * 128], IDB[:, :])
                last.then_inc(yt_done, 1)

            def hidden(i):
                n, f = i // NF, i % NF
                wait(pe, relu_done, i - 2)
                if i == 0:
                    pe.wait_ge(wts_done, 2)
                if i == 2:
                    pe.wait_ge(nmts_done, NB)
                pe.wait_ge(yts_done, n + 1)
                for j in range(DH):
                    last = mm(P_H[i % 3][:, :], W1T[:, j, f * 128:(f + 1) * 128], YT[:, n % 2, j, :],
                              start=(j == 0), stop=(j == DH - 1))
                last.then_inc(h_done, 1)
                if f == TURN[n]:
                    turn(n + 1)

            def output(k, s):
                n, f = k // NF, k % NF
                if k == s == 0:
                    pe.wait_ge(wts_done, 4)
                if k == 0 and s == 2:
                    pe.wait_ge(x1_done, NB)
                pe.wait_ge(hq_done, k + 1)
                if f == 0:
                    wait(pe, res_done, BG * (n - 1) + s + 1)
                mm(P_O[s][:, 0:D], HQ[:, n % 2, f, s * S:(s + 1) * S], W2T[:, f, :],
                   start=(f == 0), stop=(f == NF - 1)).then_inc(o_done[s], 1)

            pipeline(pe, step, head)
            for i in range(FIRST, NT + 1):
                if i < NT:
                    hidden(i)
                for k, s in parts_due[i]:
                    output(k, s)

    return nc


_INS = ['x', 'ctx_512', 'L0_xattn_Wc', 'L0_xattn_bc', 'L0_ffn_W1', 'L0_ffn_b1', 'L0_ffn_W2', 'L0_ffn_b2',
        'L0_ffn_s_act1', 'L0_ffn_s_act2']


def kernel(**inputs):
    import numpy as _np
    import concourse.bacc as _bacc
    from concourse import mybir as _mybir
    from concourse.bass_utils import run_bass_kernel_spmd as _run

    nc = _bacc.Bacc("TRN2", target_bir_lowering=False, num_devices=1)
    arrays, args = {}, []
    for name in _INS:
        a = _np.ascontiguousarray(inputs[name])
        arrays[f"in_{name}"] = a
        args.append(nc.dram_tensor(f"in_{name}", a.shape, _mybir.dt.from_np(a.dtype), kind="ExternalInput").ap())
    out = nc.dram_tensor("out_x", inputs['x'].shape, _mybir.dt.float32, kind="ExternalOutput").ap()
    xattn_ffn(nc, *args, out)
    r = _run(nc, [arrays], core_ids=[0])
    return r.results[0]["out_x"]
```
